# Optimizing a Trainium2 kernel written in Bass

```python
import numpy as np
import jax
import jax.numpy as jnp

def _softmax(x, axis=-1):
    return jax.nn.softmax(x, axis=axis)

def _gelu(x):
    return jax.nn.gelu(x, approximate=True)

def _silu(x):
    return jax.nn.silu(x)

def _sigmoid(x):
    return jax.nn.sigmoid(x)

def _layernorm(x, axis=-1, eps=1e-05):
    m = jnp.mean(x, axis=axis, keepdims=True)
    v = jnp.var(x, axis=axis, keepdims=True)
    return (x - m) / jnp.sqrt(v + eps)

def _scatter_add(tgt, idx, src, axis=0):
    return tgt.at[idx].add(src)

def _segment_sum(src, seg, n):
    return jax.ops.segment_sum(src, seg, n)
kernel_name = 'mk_adj_resnorm_d4_adj_r2_0bdf18'

def setup_inputs(seed: int=0):
    np.random.seed(seed)
    _w = jnp.asarray

    def _rec_inputs():
        import jax
        import jax.numpy as jnp
        _gk = jax.random.key(seed)
        x = -0.0003929 + 0.9999 * jax.random.normal(jax.random.fold_in(_gk, 1), (64, 128, 256), jnp.float32)
        _a = jax.random.bernoulli(jax.random.fold_in(_gk, 2), 0.0625, (64, 128, 128))
        _a = jnp.logical_or(_a, jnp.eye(128, dtype=bool))
        _af = _a.astype(jnp.float32)
        _af = _af * jax.random.uniform(jax.random.fold_in(_gk, 3), (64, 128, 128), jnp.float32, 0.05, 1)
        adj = _af
        _nm = jnp.ones((64, 128), dtype=bool)
        nodemask = jnp.where(_nm, 1.0, 0.0).astype(jnp.float32)
        return (x, adj, nodemask)
    x, adj, nodemask = _rec_inputs()

    def _L0_gnn_setup():
        import jax, jax.numpy as jnp
        import numpy as np
        EPS = 1e-06
        key = jax.random.key(seed)
        k1, k2, k3 = jax.random.split(key, 3)
        B, N, F, O = (8, 2048, 256, 256)
        x = jax.random.normal(k1, (B, N, F), dtype=jnp.float32)
        adj = jax.random.uniform(k2, (B, N, N), dtype=jnp.float32)
        W = jax.random.normal(k3, (O, 2 * F), dtype=jnp.float32) * (1.0 / np.sqrt(2 * F))
        return {'x': x, 'adj': adj, 'W': W}
    _L0_gnn_all = _L0_gnn_setup()
    _L0_gnn_in = {k: v for k, v in _L0_gnn_all.items() if k in ('W',)}
    del _L0_gnn_all

    def _L1_gnn_setup():
        import jax, jax.numpy as jnp
        import numpy as np
        B, N, DIN, DOUT, K = (4, 1024, 256, 256, 3)
        key = jax.random.key(seed)
        ks = jax.random.split(key, 8)
        X = jax.random.normal(ks[0], (B, N, DIN), dtype=jnp.float32)
        A = jax.random.uniform(ks[1], (B, N, N), dtype=jnp.float32)
        Wv = jax.random.normal(ks[2], (DIN, DOUT), dtype=jnp.float32) * 0.02
        bv = jax.random.normal(ks[3], (DOUT,), dtype=jnp.float32) * 0.02
        aw = jax.random.normal(ks[4], (2 * DOUT, 1), dtype=jnp.float32) * 0.05
        ab = jax.random.normal(ks[5], (1,), dtype=jnp.float32) * 0.05
        Wk = jax.random.normal(ks[6], (K, DIN, DOUT), dtype=jnp.float32) * 0.02
        bk = jax.random.normal(ks[7], (K, DOUT), dtype=jnp.float32) * 0.02
        return {'X': X, 'A': A, 'Wv': Wv, 'bv': bv, 'aw': aw, 'ab': ab, 'Wk': Wk, 'bk': bk}
    _L1_gnn_all = _L1_gnn_setup()
    _L1_gnn_in = {k: v for k, v in _L1_gnn_all.items() if k in ('Wv', 'bv', 'aw', 'ab', 'Wk', 'bk')}
    del _L1_gnn_all

    def _L2_gnn_setup():
        import jax, jax.numpy as jnp
        import numpy as np
        B, N, IN_DIM, ATT_DIM = (2, 4096, 256, 256)
        key = jax.random.key(seed)
        k1, k2, k3, k4 = jax.random.split(key, 4)
        X = jax.random.normal(k1, (B, N, IN_DIM), dtype=jnp.float32)
        adj = jax.random.uniform(k2, (B, N, N), dtype=jnp.float32)
        mask = jnp.ones((B, N), dtype=jnp.float32)
        Wqk = jax.random.normal(k3, (IN_DIM, 2 * ATT_DIM), dtype=jnp.float32) / np.sqrt(IN_DIM)
        Wv = jax.random.normal(k4, (IN_DIM, IN_DIM), dtype=jnp.float32) / np.sqrt(IN_DIM)
        return {'X': X, 'adj': adj, 'mask': mask, 'Wqk': Wqk, 'Wv': Wv}
    _L2_gnn_all = _L2_gnn_setup()
    _L2_gnn_in = {k: v for k, v in _L2_gnn_all.items() if k in ('Wqk', 'Wv')}
    del _L2_gnn_all

    def _L3_gnn_setup():
        import jax, jax.numpy as jnp
        import numpy as np
        IN_DIM = 256
        ATT_DIM = 64
        B, N = (4, 2048)
        key = jax.random.key(seed)
        k1, k2, k3, k4 = jax.random.split(key, 4)
        x = jax.random.normal(k1, (B, N, IN_DIM), dtype=jnp.float32)
        adj_matrix = (jax.random.uniform(k2, (B, N, N)) < 0.05).astype(jnp.float32)
        W_qk = jax.random.normal(k3, (2 * ATT_DIM, IN_DIM), dtype=jnp.float32) / np.sqrt(IN_DIM)
        W_v = jax.random.normal(k4, (IN_DIM, IN_DIM), dtype=jnp.float32) / np.sqrt(IN_DIM)
        return {'x': x, 'adj_matrix': adj_matrix, 'W_qk': W_qk, 'W_v': W_v}
    _L3_gnn_all = _L3_gnn_setup()
    _L3_gnn_in = {k: v for k, v in _L3_gnn_all.items() if k in ('W_qk', 'W_v')}
    del _L3_gnn_all
    return {'x': x, 'adj': adj, 'nodemask': nodemask, 'L0_gnn_W': _L0_gnn_in['W'], 'L1_gnn_Wv': _L1_gnn_in['Wv'], 'L1_gnn_bv': _L1_gnn_in['bv'], 'L1_gnn_aw': _L1_gnn_in['aw'], 'L1_gnn_ab': _L1_gnn_in['ab'], 'L1_gnn_Wk': _L1_gnn_in['Wk'], 'L1_gnn_bk': _L1_gnn_in['bk'], 'L2_gnn_Wqk': _L2_gnn_in['Wqk'], 'L2_gnn_Wv': _L2_gnn_in['Wv'], 'L3_gnn_W_qk': _L3_gnn_in['W_qk'], 'L3_gnn_W_v': _L3_gnn_in['W_v']}

def reference(x, adj, nodemask, L0_gnn_W, L1_gnn_Wv, L1_gnn_bv, L1_gnn_aw, L1_gnn_ab, L1_gnn_Wk, L1_gnn_bk, L2_gnn_Wqk, L2_gnn_Wv, L3_gnn_W_qk, L3_gnn_W_v):
    import jax
    import jax.numpy as jnp

    def _L0_gnn_ref(x, adj, W):
        import jax, jax.numpy as jnp
        import numpy as np
        EPS = 1e-06
        deg = jnp.sum(adj, axis=-1, keepdims=True)
        agg = jnp.einsum('bij,bjf->bif', adj, x) / jnp.maximum(deg, EPS)
        cat = jnp.concatenate([x, agg], axis=2)
        out = jnp.einsum('bnf,of->bno', cat, W)
        return jax.nn.relu(out)

    def _L1_gnn_ref(X, A, Wv, bv, aw, ab, Wk, bk):
        import jax, jax.numpy as jnp
        import numpy as np
        B, N, DIN, DOUT, K = (4, 1024, 256, 256, 3)
        d = Wv.shape[1]
        Xw = X @ Wv + bv
        sj = Xw @ aw[:d, 0]
        si = Xw @ aw[d:, 0]
        e = jax.nn.leaky_relu(sj[:, None, :] + si[:, :, None] + ab[0], negative_slope=0.2)
        alpha_matrix = A * jnp.exp(e)
        transition = alpha_matrix / (jnp.sum(alpha_matrix, axis=-1, keepdims=True) + 1e-12)
        H = jnp.zeros(X.shape[:-1] + (d,), dtype=X.dtype)
        Xk = X
        for k in range(Wk.shape[0]):
            H = H + Xk @ Wk[k] + bk[k]
            Xk = jnp.einsum('bij,bjd->bid', transition, Xk)
        return jax.nn.relu(H)

    def _L2_gnn_ref(X, adj, mask, Wqk, Wv):
        import jax, jax.numpy as jnp
        import numpy as np
        B, N, IN_DIM, ATT_DIM = (2, 4096, 256, 256)
        qk = X @ Wqk
        q, k = jnp.split(qk, 2, axis=-1)
        v = X @ Wv
        att_dim = q.shape[-1]
        inv_scale = 1.0 / jnp.sqrt(jnp.float32(att_dim))
        k_m = k * mask[:, :, None]
        agg = jnp.einsum('bij,bjd->bid', adj, k_m)
        w = inv_scale * mask * jnp.einsum('bid,bid->bi', q, agg)
        L = jax.nn.softmax(w, axis=1)[:, :, None] * v
        return L

    def _L3_gnn_ref(x, adj_matrix, W_qk, W_v):
        import jax, jax.numpy as jnp
        import numpy as np
        IN_DIM = 256
        ATT_DIM = 64
        B, N = (4, 2048)
        qk = jnp.einsum('bnd,ed->bne', x, W_qk)
        q, k = jnp.split(qk, 2, axis=-1)
        v = jnp.einsum('bnd,ed->bne', x, W_v)
        inv_scale = 1.0 / ATT_DIM ** 0.5
        scores = jnp.einsum('bnd,bmd->bnm', q, k) * inv_scale
        w = jnp.sum(scores * adj_matrix, axis=-1, keepdims=True)
        w = jax.nn.softmax(w, axis=1)
        return w * v
    x = _layernorm(x + _L0_gnn_ref(x, adj, L0_gnn_W), axis=-1)
    x = _layernorm(x + _L1_gnn_ref(x, adj, L1_gnn_Wv, L1_gnn_bv, L1_gnn_aw, L1_gnn_ab, L1_gnn_Wk, L1_gnn_bk), axis=-1)
    x = _layernorm(x + _L2_gnn_ref(x, adj, nodemask, L2_gnn_Wqk, L2_gnn_Wv), axis=-1)
    x = _layernorm(x + _L3_gnn_ref(x, adj, L3_gnn_W_qk, L3_gnn_W_v), axis=-1)
    return x

_drawn_inputs = setup_inputs


def setup_inputs(seed=0):
    import zlib

    import numpy as np

    out = dict(_drawn_inputs(seed))
    spreads = {}
    factors = {'L1_gnn_Wv': 3.575, 'L1_gnn_bv': 8.0, 'L1_gnn_aw': 3.669}
    for name, (base, spread) in spreads.items():
        noise = np.random.default_rng([zlib.crc32(name.encode()), seed]).standard_normal(out[name].shape)
        drawn = base * np.exp(spread * noise) if base else spread * noise
        out[name] = jnp.asarray(drawn.astype(out[name].dtype))
    for name, factor in factors.items():
        out[name] = (out[name] * factor).astype(out[name].dtype)
    return out
```

```python
from contextlib import ExitStack

import concourse.bass as bass
from concourse import mybir

F32 = mybir.dt.float32
F16 = mybir.dt.float16
ALU = mybir.AluOpType
ACT = mybir.ActivationFunctionType
AX_X = mybir.AxisListType.X

P = 128
G = 64
D = 256
C = D // P
ATT = 64
U = 8
QUAD = 4
SCALE = 64.0
PROD = SCALE * SCALE
DEG_EPS = 1e-6
ROW_EPS = 1e-12
LN_EPS = 1e-5
SLOPE = 0.2


N_LOADS = 12
BIAS_STEP = 7
PREP_ACT = 14
PREP_DVE = 27
QUEUE = 2


class Item:

    def __init__(self, index, pos):
        self.index, self.pos = index, pos

    def ring(self, depth):
        return self.pos % depth

    def count(self, back=0):
        return self.index + (1 - back)


class Step:
    def __init__(self, index, pos):
        self.index, self.pos = index, pos

    def item(self, offset):
        if isinstance(self.index, int) and not 0 <= self.index + offset < G:
            return None
        return Item(self.index + offset, (self.pos + offset) % U)


def run_steps(eng, lead, lag, body, first=1):
    first = max(first, -(-lag // U))
    last = (G - lead) // U
    for t in range(-lead, first * U):
        body(Step(t, t % U))
    with eng.Fori(first, last) as o:
        for v in range(U):
            body(Step(o * U + v, v))
    for t in range(last * U, G + lag):
        body(Step(t, t % U))


def wait(eng, sem, count):
    if isinstance(count, int) and count <= 0:
        return
    eng.wait_ge(sem, count)


def gnn_stack(nc, x_in, adj_in, mask_in, w0_in, wv1_in, bv1_in, aw1_in, ab1_in, wk1_in, bk1_in,
              wqk2_in, wv2_in, wqk3_in, wv3_in, out):
    with ExitStack() as ctx:
        def sb(name, shape, dt=F32):
            return ctx.enter_context(nc.sbuf_tensor(name, shape, dt))

        def sem(name):
            return ctx.enter_context(nc.semaphore(name))

        x = sb("x", [P, G, D])
        adj = sb("adj", [P, G, P])
        an_t = sb("an_t", [P, G, 2, P], F16)
        am_t = sb("am_t", [P, G, 2, P], F16)
        deg_m = sb("deg_m", [P, G])
        w0 = sb("w0", [P, C, 2 * D])
        w1 = [sb(f"w1_{h}", [P, C, 3 * D + 2], F16) for h in ("hi", "lo")]
        vj = [sb(f"vj_{h}", [P, C, P], F16) for h in ("hi", "lo")]
        bias1 = sb("bias1", [P, D], F16)
        ones1 = sb("ones1", [P, P], F16)
        w2 = [sb(f"w2_{h}", [P, C, 2 * D], F16) for h in ("hi", "lo")]
        w3 = [sb(f"w3_{h}", [P, C, 3 * P], F16) for h in ("hi", "lo")]
        mask_t = sb("mask_t", [P, G])
        logit_c = sb("logit_c", [P, G])
        logit_d = sb("logit_d", [P, G])
        score_c = sb("score_c", [P, 1])
        ident = sb("ident", [P, P])
        ident16 = sb("ident16", [P, P], F16)
        minus_half = sb("minus_half", [P, QUAD])

        stage = am_t[:].rearrange("p g h n -> p (g h n)")
        used = [0]

        def staged(words):
            a = used[0]
            used[0] += 2 * words
            assert used[0] <= G * 2 * P
            return stage[:, a:a + 2 * words].bitcast(F32)

        w0_nat = staged(C * 2 * D).rearrange("p (c f) -> p c f", c=C)
        wk_f = staged(C * 3 * D).rearrange("p (c k f) -> p c k f", c=C, k=3)
        wv1_f = staged(C * D).rearrange("p (c f) -> p c f", c=C)
        wqk2_nat = staged(C * 2 * D).rearrange("p (c f) -> p c f", c=C)
        wqk2_t = staged(4 * D).rearrange("p (a d) -> p a d", a=4)
        w2_f = staged(C * 2 * D).rearrange("p (c f) -> p c f", c=C)
        wqk3_nat = staged(D)
        w3_f = staged(C * 3 * P).rearrange("p (c f) -> p c f", c=C)
        mask_nat = staged(P)
        shared = sb("shared", [P, 2 * (P * 4 + (D + P) * 4 + D * 4)], F16)
        taken = [0, 0, 0]

        def ring_of(layer, shape, dt=F32):
            size = 2 // (1 if dt == F32 else 2)
            for n in shape:
                size *= n
            at = taken[layer]
            taken[layer] += size
            flat = shared[:, at:at + size]
            flat = flat.bitcast(F32) if dt == F32 else flat
            names = "abc"[:len(shape)]
            sizes = dict(zip(names[1:], shape[1:]))
            return flat.rearrange(f"p ({' '.join(names)}) -> p {' '.join(names)}", **sizes)

        an = ring_of(0, [4, P])
        xa = ring_of(0, [4, D + P])
        y0 = ring_of(0, [4, D])
        bcast = y0.rearrange("p r d -> p (r d)")
        wv3_nat = xa.rearrange("p r d -> p (r d)")[:, 0:C * D].rearrange("p (c f) -> p c f", c=C)
        prod = xa.rearrange("p r d -> p (r d)")[:, C * D:C * D + D]
        vcols = sb("vcols", [P, 2, C])
        bsum = sb("bsum", [P, 4])

        hi = sb("hi", [P, 4, D], F16)
        lo = sb("lo", [P, 4, D], F16)
        x_fixed = hi[:].rearrange("p r d -> p (r d)").bitcast(F32).rearrange("p (r d) -> p r d", r=2)
        xt = sb("xt", [P, 8, 4, P], F16)
        xt_f = xt[:].rearrange("p r c n -> p (r c n)").bitcast(F32)
        rows = xt_f[0:1, 0:4 * D + 2]
        bk_rows = xt_f[0:1, 4 * D + 2:7 * D + 2]
        ones_row = sb("ones_row", [1, P])
        dg = sb("dg", [P, 2, QUAD])
        rdeg = sb("rdeg", [P, 2, QUAD])
        u = ring_of(1, [2, P])
        lk = ring_of(1, [2, P])
        ex = ring_of(1, [2, P])
        alpha = ring_of(1, [2, P])
        asum = sb("asum", [P, 2, 1])
        rsum = sb("rsum", [P, 2, 1])
        rinv = sb("rinv", [P, 2, 1])
        tr = ring_of(1, [2, 2, P], F16)
        tr_t = ring_of(1, [2, 2, P], F16)
        yh = ring_of(1, [2, 2, D], F16)
        zh = ring_of(1, [2, 2, D], F16)
        hr = ring_of(1, [2, D])
        kh = ring_of(2, [2, 2, ATT], F16)
        qs = ring_of(2, [2, ATT])
        dots = sb("dots", [P, 2, QUAD])
        logits = sb("logits", [P, 2, QUAD])
        pmax = sb("pmax", [QUAD, 2, 1])
        nmax = sb("nmax", [QUAD, 2, 1])
        pexp = ring_of(2, [2, P])[0:QUAD]
        psums = sb("psums", [QUAD, 2, 1])
        pinv = sb("pinv", [QUAD, 2, 1])
        prow = ring_of(2, [2, P])[0:QUAD]
        pcol = sb("pcol", [P, 2, QUAD])
        junk = ring_of(2, [2, D])
        assert taken[2] <= taken[1] - 2 * 2 * D

        bst = sb("bst", [P, 8, 6])
        mv = sb("mv", [P, 2, QUAD, 2])
        veps = sb("veps", [P, 2, QUAD])
        rstd = sb("rstd", [P, 2, QUAD])
        nb = sb("nb", [P, 2, QUAD])

        bank = [ctx.enter_context(nc.psum_tensor(f"bank{i}", [P, 512], F32)) for i in range(8)]
        bank16 = [b[:].bitcast(F16) for b in bank]

        x_loaded = [sem(f"x_loaded{i}") for i in range(QUEUE)]
        a_loaded = [sem(f"a_loaded{i}") for i in range(QUEUE)]
        w0_loaded = sem("w0_loaded")
        w_loaded = sem("w_loaded")
        stored = sem("stored")
        ident_ready = sem("ident_ready")
        pool_ready = sem("pool_ready")
        prep_pe = sem("prep_pe")
        prep_dve = sem("prep_dve")
        prep_act = sem("prep_act")

        deg_done = sem("deg_done")
        degm_done = sem("degm_done")
        rdeg_done = sem("rdeg_done")
        x_fixed_done = sem("x_fixed_done")
        an_done = sem("an_done")
        tr0_done = sem("tr0_done")
        xa_done = sem("xa_done")
        ahi_done = sem("ahi_done")
        alo_done = sem("alo_done")
        xw0_done = sem("xw0_done")
        y0_done = sem("y0_done")
        ay_done = sem("ay_done")

        coef_done = sem("coef_done")
        hi_done = [None] + [sem(f"hi_done{n}") for n in (1, 2, 3)]
        lo_done = [None] + [sem(f"lo_done{n}") for n in (1, 2, 3)]
        trx_done = [None] + [sem(f"trx_done{n}") for n in (1, 2, 3)]
        xt_done = [None] + [sem(f"xt_done{n}") for n in (1, 2, 3)]

        xwb_done = sem("xwb_done")
        xwa_done = sem("xwa_done")
        u_done = sem("u_done")
        lk_done = sem("lk_done")
        ex_done = sem("ex_done")
        alpha_done = sem("alpha_done")
        rsum_done = sem("rsum_done")
        rinv_done = sem("rinv_done")
        thi_done = sem("thi_done")
        tlo_done = sem("tlo_done")
        trt_done = sem("trt_done")
        tt_done = sem("tt_done")
        yhi_done = sem("yhi_done")
        ylo_done = sem("ylo_done")
        ty_done = sem("ty_done")
        zhi_done = sem("zhi_done")
        zlo_done = sem("zlo_done")
        tz_done = sem("tz_done")
        relu_done = sem("relu_done")

        qx_done = [None, None, sem("xm_done"), sem("qk_done")]
        ax_done = [None, None, sem("ax_done"), sem("ak_done")]
        q_saved = [None, None, sem("xm_saved"), sem("q_saved")]
        khi_done = sem("khi_done")
        klo_done = sem("klo_done")
        dot_done = [None, None, sem("dot_done2"), sem("dot_done3")]
        logit_done = [None, None, sem("logit_done2"), sem("logit_done3")]
        turned = [None, None, sem("turned2"), sem("turned3")]
        pmax_done = [None, None, sem("pmax_done2"), sem("pmax_done3")]
        nmax_done = [None, None, sem("nmax_done2"), sem("nmax_done3")]
        pexp_done = [None, None, sem("pexp_done2"), sem("pexp_done3")]
        pinv_done = [None, None, sem("pinv_done2"), sem("pinv_done3")]
        prow_done = [None, None, sem("prow_done2"), sem("prow_done3")]
        pback = [None, None, sem("pback2"), sem("pback3")]
        pcol_done = [None, None, sem("pcol_done2"), sem("pcol_done3")]
        v_done = [None, None, sem("v_done2"), sem("v_done3")]

        res_done = [sem(f"res_done{n}") for n in range(4)]
        stats_done = [sem(f"stats_done{n}") for n in range(4)]
        aggr_done = [sem(f"aggr_done{n}") for n in range(4)]
        veps_done = [sem(f"veps_done{n}") for n in range(4)]
        rstd_done = [sem(f"rstd_done{n}") for n in range(4)]
        nb_done = [sem(f"nb_done{n}") for n in range(4)]
        norm_done = [sem(f"norm_done{n}") for n in range(4)]

        xt_last = [None, xwa_done, v_done[2], v_done[3]]
        RES_LAG = [1, 1, 6, 6]
        NORM_LAG = [r + 6 for r in RES_LAG]

        block = ctx.enter_context(nc.Block())

        @block.sync
        def _(sp):
            def load(q, i):
                sp.dma_start(adj[:, bass.ds(q * QUAD, QUAD), :],
                             adj_in[bass.ds(q * QUAD, QUAD)].rearrange("g n m -> n g m"))\
                    .then_inc(a_loaded[i], 16)
                sp.dma_start(x[:, bass.ds(q * QUAD, QUAD), :],
                             x_in[bass.ds(q * QUAD, QUAD)].rearrange("g n d -> n g d"))\
                    .then_inc(x_loaded[i], 16)

            for i in range(QUEUE):
                load(i, i)
            with sp.Fori(1, G // QUAD // QUEUE) as r:
                for i in range(QUEUE):
                    sp.wait_ge(a_loaded[i], 16 * r)
                    sp.wait_ge(x_loaded[i], 16 * r)
                    load(r * QUEUE + i, i)
            with sp.Fori(0, G // 2) as h:
                sp.wait_ge(norm_done[3], 2 * h + 2)
                sp.dma_start(out[bass.ds(h * 2, 2)].rearrange("g n d -> n g d"),
                             x[:, bass.ds(h * 2, 2), :]).then_inc(stored, 16)
            sp.wait_ge(stored, 16 * (G // 2))

        @block.gpsimd
        def _(pool):
            nc.gpsimd.memset(ident[:], 0.0).then_inc(ident_ready, 1)
            nc.gpsimd.memset(ident16[:], 0.0).then_inc(ident_ready, 1)
            pool.wait_ge(ident_ready, 2)
            for m in (ident, ident16):
                nc.gpsimd.affine_select(out=m[:], in_=m[:], compare_op=ALU.not_equal, fill=1.0, base=0,
                                        pattern=[[-1, P]], channel_multiplier=1).then_inc(ident_ready, 1)
            nc.gpsimd.memset(minus_half[:], -0.5).then_inc(pool_ready, 1)
            pool.wait_ge(pool_ready, 1)
            nc.gpsimd.tensor_tensor(rstd[:, 0, :], minus_half[:], minus_half[:], ALU.mult).then_inc(pool_ready, 1)
            pool.wait_ge(pool_ready, 2)

            def inverse_root(n, g):
                if g is None or g.pos % QUAD != QUAD - 1:
                    return
                r = g.ring(8) // QUAD
                wait(pool, veps_done[n], g.count())
                if n and isinstance(g.index, int) and g.index < U:
                    pool.wait_ge(norm_done[n - 1], G)
                wait(pool, norm_done[n], g.count(8))
                nc.gpsimd.tensor_tensor(rstd[:, r, :], veps[:, r, :], minus_half[:], ALU.pow)\
                    .then_inc(rstd_done[n], QUAD)

            def step0(s):
                if g := s.item(3):
                    if g.pos % QUAD == 0:
                        pool.wait_ge(x_loaded[g.pos // QUAD], (g.index - g.pos) * 2 + 16)
                    wait(pool, tr0_done, g.count(2))
                    nc.gpsimd.tensor_copy(x_fixed[:, g.ring(2), :], x[:, g.index, :])\
                        .then_inc(x_fixed_done, 1)
                inverse_root(0, s.item(-RES_LAG[0] - 1))

            run_steps(pool, 3, RES_LAG[0] + 1, step0, first=2)

            for n in (1, 2, 3):
                lead = 4 if n == 1 else 3

                def step(s, n=n, lead=lead):
                    if g := s.item(lead):
                        wait(pool, hi_done[n], g.count())
                        wait(pool, (trx_done if n == 1 else ax_done if n == 2 else trx_done)[n], g.count(4))
                        nc.gpsimd.tensor_tensor(lo[:, g.ring(4), :], x[:, g.index, :], hi[:, g.ring(4), :],
                                                ALU.subtract).then_inc(lo_done[n], 1)
                    inverse_root(n, s.item(-RES_LAG[n] - 1))

                run_steps(pool, lead, RES_LAG[n] + 1, step, first=2)

        @block.scalar
        def _(act):
            act.dma_start(w0_nat, w0_in.rearrange("(c p) f -> p c f", p=P)).then_inc(w0_loaded, 16)
            act.dma_start(mask_nat[0:G, :], mask_in).then_inc(w0_loaded, 16)
            loads = [
                (rows[:, 0:2 * D], aw1_in.rearrange("(a n) -> a n", a=1)),
                (rows[:, 2 * D:3 * D], bv1_in.rearrange("(a n) -> a n", a=1)),
                (rows[:, 4 * D:4 * D + 1], ab1_in.rearrange("(a n) -> a n", a=1)),
                (bk_rows, bk1_in.rearrange("(a k) n -> a (k n)", a=1)),
                (wv1_f, wv1_in.rearrange("(c p) f -> p c f", p=P)),
                (wqk2_nat, wqk2_in.rearrange("(c p) f -> p c f", p=P)),
                (w2_f[:, :, D:2 * D], wv2_in.rearrange("(c p) f -> p c f", p=P)),
                (wqk3_nat, wqk3_in),
                (wv3_nat, wv3_in.rearrange("(c p) f -> p c f", p=P)),
            ] + [(wk_f[:, :, k, :], wk1_in[k].rearrange("(c p) f -> p c f", p=P)) for k in range(3)]
            for dst, src in loads:
                act.dma_start(dst, src).then_inc(w_loaded, 16)
            assert len(loads) == N_LOADS
            nc.scalar.preload_act_table(ACT.Exp)

            act.wait_ge(prep_pe, 1)
            nc.scalar.activation(w0[:, 0, :], bank[0][:], ACT.Copy).then_inc(prep_act, 1)
            nc.scalar.activation(w0[:, 1, :], bank[1][:], ACT.Copy).then_inc(prep_act, 1)
            nc.scalar.activation(mask_t[:], bank[7][:, 0:G], ACT.Copy).then_inc(prep_act, 1)
            act.wait_ge(prep_pe, 2)
            nc.scalar.activation(wqk2_t[:, 0:2, :].rearrange("p a d -> p (a d)"), bank[2][:], ACT.Copy)\
                .then_inc(prep_act, 1)
            nc.scalar.activation(wqk2_t[:, 2:4, :].rearrange("p a d -> p (a d)"), bank[3][:], ACT.Copy)\
                .then_inc(prep_act, 1)
            act.wait_ge(prep_pe, 3)
            nc.scalar.activation(w3_f[:, :, 0:P], bank[5][:, 0:C * P].rearrange("p (c e) -> p c e", c=C),
                                 ACT.Copy).then_inc(prep_act, 1)
            nc.scalar.activation(w3_f[:, :, P:3 * P], bank[6][:].rearrange("p (c e) -> p c e", c=C),
                                 ACT.Copy).then_inc(prep_act, 1)
            act.wait_ge(prep_pe, 4)
            nc.scalar.activation(w2_f[:, :, 0:D], bank[4][:].rearrange("p (c e) -> p c e", c=C),
                                 ACT.Copy).then_inc(prep_act, 1)
            act.wait_ge(prep_pe, 5)
            nc.scalar.activation(bcast[:, 0:2 * D], bank[0][:], ACT.Copy).then_inc(prep_act, 1)
            nc.scalar.activation(bcast[:, 2 * D:4 * D], bank[1][:], ACT.Copy).then_inc(prep_act, 1)
            nc.scalar.activation(bsum[:, 3:4], bank[2][:, 0:1], ACT.Copy).then_inc(prep_act, 1)
            act.wait_ge(w_loaded, 16 * N_LOADS)
            nc.scalar.activation(w1[0][:, :, 0:3 * D], wk_f.rearrange("p c k f -> p c (k f)"), ACT.Copy,
                                 scale=SCALE).then_inc(prep_act, 1)
            act.wait_ge(prep_act, 8)
            nc.scalar.activation(w2[0][:], w2_f, ACT.Copy, scale=SCALE).then_inc(prep_act, 1)
            nc.scalar.activation(w3[0][:], w3_f, ACT.Copy, scale=SCALE).then_inc(prep_act, 1)
            act.wait_ge(prep_act, PREP_ACT)
            act.wait_ge(prep_dve, PREP_DVE)

            def step0(s):
                if g := s.item(2):
                    wait(act, tr0_done, g.count())
                    wait(act, ay_done, g.count(4))
                    nc.scalar.activation(xa[:, g.ring(4), :], bank[g.ring(2)][:, 0:D + P], ACT.Copy)\
                        .then_inc(xa_done, 1)
                    nc.scalar.activation(an_t[:, g.index, 0, :], bank[g.ring(2)][:, D:D + P], ACT.Copy)
                    nc.scalar.activation(am_t[:, g.index, 0, :], bank[g.ring(2)][:, D:D + P], ACT.Copy,
                                         scale=mask_t[:, bass.ds(g.index, 1)]).then_inc(ahi_done, 1)
                if g := s.item(0):
                    wait(act, xw0_done, g.count())
                    nc.scalar.activation(y0[:, g.ring(4), :], bank[2 + g.ring(4)][:, D:2 * D], ACT.Copy,
                                         scale=1.0 / SCALE).then_inc(y0_done, 1)

            run_steps(act, 2, 0, step0)

            def split_hi(n, g):
                wait(act, norm_done[n - 1], g.count())
                wait(act, (trx_done if n != 2 else ax_done)[n], g.count(4))
                if n > 1 and isinstance(g.index, int) and g.index < 4:
                    act.wait_ge((trx_done if n != 3 else ax_done)[n - 1], G)
                nc.scalar.activation(hi[:, g.ring(4), :], x[:, g.index, :], ACT.Copy).then_inc(hi_done[n], 1)

            def save_xt(n, g, last_reader, depth=8):
                wait(act, trx_done[n], g.count())
                wait(act, last_reader[n], g.count(depth))
                if n > 1 and isinstance(g.index, int) and g.index < depth:
                    act.wait_ge(last_reader[n - 1], G)
                nc.scalar.activation(xt[:, g.ring(8), :, :].rearrange("p c n -> p (c n)"),
                                     bank16[g.ring(2)][:, 0:4 * P], ACT.Copy).then_inc(xt_done[n], 1)

            def step1(s):
                if g := s.item(-1):
                    wait(act, tz_done, g.count())
                    wait(act, res_done[1], g.count(2))
                    nc.scalar.activation(hr[:, g.ring(2), :], bank[4 + g.ring(2)][:, 0:D], ACT.Relu,
                                         scale=1.0 / SCALE).then_inc(relu_done, 1)
                if g := s.item(0):
                    wait(act, trt_done, g.count())
                    wait(act, tz_done, g.count(2))
                    nc.scalar.activation(tr_t[:, g.ring(2), :, :].rearrange("p h n -> p (h n)"),
                                         bank16[6 + g.ring(2)][:, 0:2 * P], ACT.Copy).then_inc(tt_done, 1)
                if g := s.item(3):
                    save_xt(1, g, xt_last)
                if g := s.item(4):
                    split_hi(1, g)
                if g := s.item(0):
                    wait(act, ty_done, g.count())
                    nc.scalar.activation(zh[:, g.ring(2), 0, :], bank[4 + g.ring(2)][:, D:2 * D], ACT.Copy,
                                         scale=1.0 / SCALE).then_inc(zhi_done, 1)
                if g := s.item(2):
                    wait(act, u_done, g.count())
                    wait(act, ty_done, g.count(2))
                    nc.scalar.activation(yh[:, g.ring(2), 0, :], bank[2 + g.ring(2)][:, 0:D], ACT.Copy,
                                         scale=1.0 / SCALE).then_inc(yhi_done, 1)
                    wait(act, lk_done, g.count())
                    wait(act, alpha_done, g.count(2))
                    nc.scalar.activation(ex[:, g.ring(2), :], lk[:, g.ring(2), :], ACT.Exp,
                                         scale=1.0 / PROD).then_inc(ex_done, 1)

            run_steps(act, 4, 1, step1)

            def softmax_exp(n, g):
                r = g.ring(8) // QUAD
                wait(act, nmax_done[n], g.count())
                wait(act, pback[n], g.count(8))
                if n == 3 and isinstance(g.index, int) and g.index < U:
                    act.wait_ge(pback[2], G)
                nc.scalar.activation(pexp[:, r, :], bank[7][0:QUAD, 0:P], ACT.Exp, bias=nmax[:, r, :],
                                     accum_out=psums[:, r, :]).then_inc(pexp_done[n], QUAD)

            def step2(s):
                if g := s.item(3):
                    split_hi(2, g)
                if g := s.item(2):
                    save_xt(2, g, xt_last)
                if g := s.item(1):
                    wait(act, qx_done[2], g.count())
                    wait(act, dot_done[2], g.count(2))
                    if isinstance(g.index, int) and g.index < 2:
                        act.wait_ge(res_done[1], G)
                    nc.scalar.activation(hr[:, g.ring(2), :], bank[2 + g.ring(2)][:, 0:D], ACT.Copy)\
                        .then_inc(q_saved[2], 1)
                if (g := s.item(-1)) and g.pos % QUAD == QUAD - 1:
                    softmax_exp(2, g)

            run_steps(act, 3, 1, step2, first=2)

            def step3(s):
                if g := s.item(3):
                    split_hi(3, g)
                if g := s.item(2):
                    save_xt(3, g, xt_last)
                if g := s.item(1):
                    wait(act, qx_done[3], g.count())
                    wait(act, dot_done[3], g.count(2))
                    nc.scalar.activation(qs[:, g.ring(2), :], bank[2 + g.ring(2)][:, 0:ATT], ACT.Copy)\
                        .then_inc(q_saved[3], 1)
                    nc.scalar.activation(kh[:, g.ring(2), 0, :], bank[2 + g.ring(2)][:, ATT:2 * ATT], ACT.Copy,
                                         scale=1.0 / SCALE).then_inc(khi_done, 1)
                if (g := s.item(-1)) and g.pos % QUAD == QUAD - 1:
                    softmax_exp(3, g)

            run_steps(act, 3, 1, step3, first=2)

        @block.vector
        def _(dve):
            done = [0]

            def prep(ins):
                done[0] += 1
                ins.then_inc(prep_dve, 1)
                dve.wait_ge(prep_dve, done[0])

            v = nc.vector
            prep(v.memset(ones1[:], 1.0))
            prep(v.memset(ones_row[:], 1.0))
            prep(v.memset(rows[:, 4 * D + 1:4 * D + 2], 0.0))
            for w in w1:
                prep(v.memset(w[:, :, 3 * D:3 * D + 2], 0.0))
            dve.wait_ge(w_loaded, 16 * N_LOADS)
            prep(v.tensor_tensor(bk_rows[:, 0:D], bk_rows[:, 0:D], bk_rows[:, D:2 * D], ALU.add))
            prep(v.tensor_tensor(rows[:, 3 * D:4 * D], bk_rows[:, 0:D], bk_rows[:, 2 * D:3 * D], ALU.add))
            assert done[0] == BIAS_STEP
            dve.wait_ge(prep_act, 11)
            for j in range(2):
                for c in range(C):
                    prep(v.scalar_tensor_tensor(out=prod, in0=wv1_f[:, c, :], scalar=SCALE,
                                                in1=bcast[:, j * D:(j + 1) * D], op0=ALU.mult, op1=ALU.mult,
                                                accum_out=vcols[:, j, c:c + 1]))
                prep(v.scalar_tensor_tensor(out=prod, in0=bcast[:, 2 * D:3 * D], scalar=1.0,
                                            in1=bcast[:, j * D:(j + 1) * D], op0=ALU.mult, op1=ALU.mult,
                                            accum_out=bsum[:, j:j + 1]))
            prep(v.tensor_tensor(bsum[:, 2:3], bsum[:, 0:1], bsum[:, 1:2], ALU.add))
            prep(v.tensor_scalar(score_c[:], bsum[:, 2:3], bsum[:, 3:4], PROD, ALU.add, ALU.mult))
            prep(v.tensor_copy(w1[0][:, :, 3 * D], vcols[:, 1, :]))
            prep(v.tensor_tensor(w1[1][:, :, 3 * D], vcols[:, 1, :], w1[0][:, :, 3 * D], ALU.subtract))
            for c in range(C):
                prep(v.tensor_scalar(vj[0][:, c, :], ones1[:], vcols[:, 0, c:c + 1], None, ALU.mult))
                prep(v.scalar_tensor_tensor(out=vj[1][:, c, :], in0=ones1[:], scalar=vcols[:, 0, c:c + 1],
                                            in1=vj[0][:, c, :], op0=ALU.mult, op1=ALU.subtract))
            prep(v.tensor_scalar(bias1[:], bcast[:, 3 * D:4 * D], SCALE, None, ALU.mult))
            prep(v.tensor_copy(prod[P // 2:P, :], bias1[P // 2:P, :]))
            prep(v.scalar_tensor_tensor(out=bias1[P // 2:P, :], in0=bcast[P // 2:P, 3 * D:4 * D], scalar=SCALE,
                                        in1=prod[P // 2:P, :], op0=ALU.mult, op1=ALU.subtract))
            dve.wait_ge(prep_act, PREP_ACT)
            prep(v.scalar_tensor_tensor(out=w1[1][:, :, 0:3 * D], in0=wk_f.rearrange("p c k f -> p c (k f)"),
                                        scalar=SCALE, in1=w1[0][:, :, 0:3 * D], op0=ALU.mult, op1=ALU.subtract))
            prep(v.scalar_tensor_tensor(out=w2[1][:], in0=w2_f, scalar=SCALE, in1=w2[0][:],
                                        op0=ALU.mult, op1=ALU.subtract))
            prep(v.scalar_tensor_tensor(out=w3[1][:], in0=w3_f, scalar=SCALE, in1=w3[0][:],
                                        op0=ALU.mult, op1=ALU.subtract))
            assert done[0] == PREP_DVE, done

            def norm_stats(n, s):
                if g := s.item(-RES_LAG[n]):
                    dve.wait_ge(prep_dve, PREP_DVE)
                    wait(dve, res_done[n], g.count())
                    v.bn_stats(bst[:, g.ring(8), :], x[:, g.index, :]).then_inc(stats_done[n], 1)

            def norm_aggr(n, s):
                scale2 = 1.0 if n == 0 else PROD
                to = 1.0 / PROD if n < 3 else 1.0
                if g := s.item(-RES_LAG[n] - 1):
                    dve.wait_ge(prep_dve, PREP_DVE)
                    wait(dve, stats_done[n], g.count())
                    v.bn_aggr(mv[:, g.ring(8) // QUAD, g.ring(QUAD), :], bst[:, g.ring(8), :])\
                        .then_inc(aggr_done[n], 1)
                    if g.pos % QUAD == QUAD - 1:
                        r = g.ring(8) // QUAD
                        wait(dve, aggr_done[n], g.count())
                        v.tensor_scalar(veps[:, r, :], mv[:, r, :, 1], scale2 * LN_EPS, to, ALU.add, ALU.mult)\
                            .then_inc(veps_done[n], QUAD)

            def norm_apply(n, s):
                if (g := s.item(-RES_LAG[n] - 2)) and g.pos % QUAD == QUAD - 1:
                    r = g.ring(8) // QUAD
                    wait(dve, rstd_done[n], g.count())
                    v.scalar_tensor_tensor(out=nb[:, r, :], in0=mv[:, r, :, 0], scalar=-1.0,
                                           in1=rstd[:, r, :], op0=ALU.mult, op1=ALU.mult)\
                        .then_inc(nb_done[n], QUAD)
                if g := s.item(-NORM_LAG[n]):
                    r, k = g.ring(8) // QUAD, g.ring(QUAD)
                    wait(dve, nb_done[n], g.count(-(QUAD - 1 - k)))
                    v.tensor_scalar(x[:, g.index, :], x[:, g.index, :], rstd[:, r, k:k + 1],
                                    nb[:, r, k:k + 1], ALU.mult, ALU.add).then_inc(norm_done[n], 1)

            def norm_tail(n, s):
                norm_aggr(n, s)
                norm_stats(n, s)
                norm_apply(n, s)

            def step0(s):
                if g := s.item(-1):
                    wait(dve, ay_done, g.count())
                    v.scalar_tensor_tensor(out=x[:, g.index, :], in0=bank[2 + g.ring(4)][:, 0:D], scalar=0.0,
                                           in1=x[:, g.index, :], op0=ALU.max, op1=ALU.add)\
                        .then_inc(res_done[0], 1)
                norm_tail(0, s)
                if (g := s.item(4)) and g.pos % QUAD == 0:
                    r = g.pos // QUAD
                    cols = bass.ds(g.index, QUAD)
                    dve.wait_ge(a_loaded[r], (g.index - g.pos) * 2 + 16)
                    v.tensor_reduce(dg[:, r, :], adj[:, cols, :], AX_X, ALU.add).then_inc(deg_done, QUAD)
                    wait(dve, deg_done, g.count(1 - QUAD))
                    v.tensor_scalar(deg_m[:, cols], dg[:, r, :], DEG_EPS, None, ALU.max)\
                        .then_inc(degm_done, QUAD)
                    wait(dve, degm_done, g.count(1 - QUAD))
                    v.reciprocal(rdeg[:, r, :], deg_m[:, cols]).then_inc(rdeg_done, QUAD)
                if g := s.item(3):
                    r, k = g.pos // QUAD, g.pos % QUAD
                    wait(dve, rdeg_done, g.count(k + 1 - QUAD))
                    wait(dve, tr0_done, g.count(4))
                    v.tensor_scalar(an[:, g.ring(4), :], adj[:, g.index, :], rdeg[:, r, k:k + 1], SCALE,
                                    ALU.mult, ALU.mult).then_inc(an_done, 1)
                if g := s.item(2):
                    wait(dve, ahi_done, g.count())
                    a_t = bank[g.ring(2)][:, D:D + P]
                    v.tensor_tensor(an_t[:, g.index, 1, :], a_t, an_t[:, g.index, 0, :], ALU.subtract)
                    v.scalar_tensor_tensor(out=am_t[:, g.index, 1, :], in0=a_t,
                                           scalar=mask_t[:, bass.ds(g.index, 1)], in1=am_t[:, g.index, 0, :],
                                           op0=ALU.mult, op1=ALU.subtract).then_inc(alo_done, 1)

            run_steps(dve, 4, NORM_LAG[0], step0)

            def step1(s):
                if s.pos == 0 and (g := s.item(-2)):
                    wait(dve, res_done[1], g.count())
                norm_apply(1, s)
                norm_aggr(1, s)
                if g := s.item(1):
                    r = g.ring(2)
                    wait(dve, ex_done, g.count())
                    v.scalar_tensor_tensor(out=alpha[:, r, :], in0=adj[:, g.index, :], scalar=1.0,
                                           in1=ex[:, r, :], op0=ALU.mult, op1=ALU.mult,
                                           accum_out=asum[:, r, :]).then_inc(alpha_done, 1)
                    wait(dve, yhi_done, g.count())
                    v.scalar_tensor_tensor(out=yh[:, r, 1, :], in0=bank[2 + r][:, 0:D], scalar=1.0 / SCALE,
                                           in1=yh[:, r, 0, :], op0=ALU.mult, op1=ALU.subtract)\
                        .then_inc(ylo_done, 1)
                    wait(dve, alpha_done, g.count())
                    v.tensor_scalar(rsum[:, r, :], asum[:, r, :], ROW_EPS, 1.0 / SCALE, ALU.add, ALU.mult)\
                        .then_inc(rsum_done, 1)
                if g := s.item(-1):
                    wait(dve, relu_done, g.count())
                    v.tensor_tensor(x[:, g.index, :], x[:, g.index, :], hr[:, g.ring(2), :], ALU.add)\
                        .then_inc(res_done[1], 1)
                if g := s.item(1):
                    r = g.ring(2)
                    wait(dve, rsum_done, g.count())
                    v.reciprocal(rinv[:, r, :], rsum[:, r, :]).then_inc(rinv_done, 1)
                    wait(dve, rinv_done, g.count())
                    v.tensor_scalar(tr[:, r, 0, :], alpha[:, r, :], rinv[:, r, :], None, ALU.mult)\
                        .then_inc(thi_done, 1)
                if g := s.item(2):
                    xwb = bank[2 + g.ring(2)]
                    wait(dve, xwb_done, g.count())
                    v.tensor_scalar(u[:, g.ring(2), :], xwb[:, D + 2:D + 2 + P], xwb[:, D:D + 1],
                                    score_c[:, 0:1], ALU.add, ALU.add).then_inc(u_done, 1)
                if g := s.item(1):
                    r = g.ring(2)
                    wait(dve, thi_done, g.count())
                    v.scalar_tensor_tensor(out=tr[:, r, 1, :], in0=alpha[:, r, :], scalar=rinv[:, r, :],
                                           in1=tr[:, r, 0, :], op0=ALU.mult, op1=ALU.subtract)\
                        .then_inc(tlo_done, 1)
                if g := s.item(2):
                    wait(dve, u_done, g.count())
                    v.scalar_tensor_tensor(out=lk[:, g.ring(2), :], in0=u[:, g.ring(2), :], scalar=SLOPE,
                                           in1=u[:, g.ring(2), :], op0=ALU.mult, op1=ALU.max)\
                        .then_inc(lk_done, 1)
                if g := s.item(0):
                    wait(dve, zhi_done, g.count())
                    v.scalar_tensor_tensor(out=zh[:, g.ring(2), 1, :], in0=bank[4 + g.ring(2)][:, D:2 * D],
                                           scalar=1.0 / SCALE, in1=zh[:, g.ring(2), 0, :],
                                           op0=ALU.mult, op1=ALU.subtract).then_inc(zlo_done, 1)
                norm_stats(1, s)

            run_steps(dve, 2, NORM_LAG[1], step1)

            v.tensor_scalar(logit_d[:], deg_m[:], 1.0 / (8 * PROD * PROD), None, ALU.mult)\
                .then_inc(coef_done, 1)
            v.scalar_tensor_tensor(out=logit_c[:], in0=deg_m[:], scalar=1.0 / (16 * PROD * PROD),
                                   in1=mask_t[:], op0=ALU.mult, op1=ALU.mult).then_inc(coef_done, 1)
            dve.wait_ge(coef_done, 2)

            def gate_steps(n, width, s):
                if (g := s.item(-3)) and g.pos % QUAD == QUAD - 1:
                    r = g.ring(8) // QUAD
                    wait(dve, pback[n], g.count())
                    v.tensor_copy(pcol[:, r, :], bank[7][:, P:P + QUAD]).then_inc(pcol_done[n], QUAD)
                if (g := s.item(-2)) and g.pos % QUAD == QUAD - 1:
                    r = g.ring(8) // QUAD
                    wait(dve, pexp_done[n], g.count())
                    v.reciprocal(pinv[:, r, :], psums[:, r, :]).then_inc(pinv_done[n], QUAD)
                    wait(dve, pinv_done[n], g.count())
                    v.tensor_scalar(prow[:, r, :], pexp[:, r, :], pinv[:, r, :], 1.0 / SCALE,
                                    ALU.mult, ALU.mult).then_inc(prow_done[n], QUAD)
                if g := s.item(-RES_LAG[n]):
                    r, k = g.ring(8) // QUAD, g.ring(QUAD)
                    wait(dve, v_done[n], g.count())
                    wait(dve, pcol_done[n], g.count(k + 1 - QUAD))
                    v.scalar_tensor_tensor(out=x[:, g.index, :], in0=bank[4 + g.ring(2)][:, 0:D],
                                           scalar=pcol[:, r, k:k + 1], in1=x[:, g.index, :],
                                           op0=ALU.mult, op1=ALU.add).then_inc(res_done[n], 1)
                norm_tail(n, s)
                if (g := s.item(-1)) and g.pos % QUAD == QUAD - 1:
                    r = g.ring(8) // QUAD
                    wait(dve, turned[n], g.count())
                    v.tensor_reduce(pmax[:, r, :], bank[7][0:QUAD, 0:P], AX_X, ALU.max)\
                        .then_inc(pmax_done[n], QUAD)
                    wait(dve, pmax_done[n], g.count())
                    v.tensor_scalar(nmax[:, r, :], pmax[:, r, :], -1.0, None, ALU.mult)\
                        .then_inc(nmax_done[n], QUAD)
                if n == 3 and (g := s.item(1)):
                    wait(dve, khi_done, g.count())
                    v.scalar_tensor_tensor(out=kh[:, g.ring(2), 1, :], in0=bank[2 + g.ring(2)][:, ATT:2 * ATT],
                                           scalar=1.0 / SCALE, in1=kh[:, g.ring(2), 0, :],
                                           op0=ALU.mult, op1=ALU.subtract).then_inc(klo_done, 1)
                if g := s.item(0):
                    r, k = g.ring(8) // QUAD, g.ring(QUAD)
                    wait(dve, ax_done[n], g.count())
                    wait(dve, q_saved[n], g.count())
                    v.scalar_tensor_tensor(out=junk[:, g.ring(2), 0:width],
                                           in0=bank[2 + g.ring(2)][:, D:D + width], scalar=1.0,
                                           in1=(hr if n == 2 else qs)[:, g.ring(2), :],
                                           op0=ALU.mult, op1=ALU.mult, accum_out=dots[:, r, k:k + 1])\
                        .then_inc(dot_done[n], 1)
                    if k == QUAD - 1:
                        wait(dve, dot_done[n], g.count())
                        v.tensor_tensor(logits[:, r, :], dots[:, r, :],
                                        (logit_c if n == 2 else logit_d)[:, bass.ds(g.index - k, QUAD)],
                                        ALU.mult).then_inc(logit_done[n], QUAD)

            run_steps(dve, 0, NORM_LAG[2], lambda s: gate_steps(2, D, s))
            run_steps(dve, 1, NORM_LAG[3], lambda s: gate_steps(3, ATT, s))

        @block.tensor
        def _(pe):
            pe.wait_ge(ident_ready, 4)
            pe.wait_ge(w0_loaded, 32)

            for c in range(C):
                for half in range(2):
                    for o in range(2):
                        at = half * D + o * P
                        nc.tensor.transpose(bank[c][:, at:at + P],
                                            w0_nat[:, o, half * D + c * P:half * D + (c + 1) * P], ident[:])
            nc.tensor.transpose(bank[7][:, 0:G], mask_nat[0:G, :], ident[0:G, 0:G]).then_inc(prep_pe, 1)
            pe.wait_ge(w_loaded, 16 * N_LOADS)
            for a in range(4):
                for c in range(C):
                    at = (a % 2) * D + c * P
                    t = nc.tensor.transpose(bank[2 + a // 2][:, at:at + P],
                                            wqk2_nat[:, c, a * P:(a + 1) * P], ident[:])
            t.then_inc(prep_pe, 1)
            for c in range(C):
                nc.tensor.transpose(bank[5][:, c * P:(c + 1) * P], wqk3_nat[:, c * P:(c + 1) * P], ident[:])
                for o in range(2):
                    at = c * D + o * P
                    t = nc.tensor.transpose(bank[6][:, at:at + P], wv3_nat[:, o, c * P:(c + 1) * P], ident[:])
            t.then_inc(prep_pe, 1)
            pe.wait_ge(prep_act, 5)
            for c in range(C):
                for a in range(2):
                    t = nc.tensor.matmul(bank[4][:, c * D:(c + 1) * D], wqk2_t[:, a, c * P:(c + 1) * P],
                                         wqk2_t[:, 2 + a, :], start=(c == 0 and a == 0), stop=(a == 1),
                                         skip_group_check=True)
            t.then_inc(prep_pe, 1)
            pe.wait_ge(prep_dve, BIAS_STEP)
            nc.tensor.matmul(bank[0][:], ones_row[:], rows[:, 0:2 * D], start=True, stop=True)
            nc.tensor.matmul(bank[1][:], ones_row[:], rows[:, 2 * D:4 * D], start=True, stop=True)
            nc.tensor.matmul(bank[2][:, 0:2], ones_row[:], rows[:, 4 * D:4 * D + 2], start=True, stop=True)\
                .then_inc(prep_pe, 1)
            pe.wait_ge(prep_act, 11)

            def split_product(dst, left, right, first, last=True):
                for n, (a, b) in enumerate(((0, 0), (0, 1), (1, 0))):
                    m = nc.tensor.matmul(dst, left(a), right(b), start=first and n == 0, stop=last and n == 2,
                                         skip_group_check=True)
                return m

            def step0(s):
                if g := s.item(2):
                    wait(pe, x_fixed_done, g.count())
                    wait(pe, an_done, g.count())
                    wait(pe, alo_done, g.count(2))
                    b = bank[g.ring(2)]
                    for c in range(C):
                        nc.tensor.transpose(b[:, c * P:(c + 1) * P], x_fixed[:, g.ring(2), c * P:(c + 1) * P],
                                            ident[:])
                    nc.tensor.transpose(b[:, D:D + P], an[:, g.ring(4), :], ident[:]).then_inc(tr0_done, 1)
                if g := s.item(1):
                    wait(pe, xa_done, g.count())
                    wait(pe, res_done[0], g.count(4))
                    for c in range(C):
                        m = nc.tensor.matmul(bank[2 + g.ring(4)][:], xa[:, g.ring(4), c * P:(c + 1) * P],
                                             w0[:, c, :], start=(c == 0), stop=False, skip_group_check=True)
                    m.then_inc(xw0_done, 1)
                if g := s.item(0):
                    wait(pe, y0_done, g.count())
                    nc.tensor.matmul(bank[2 + g.ring(4)][:, 0:D], xa[:, g.ring(4), D:D + P], y0[:, g.ring(4), :],
                                     start=False, stop=True, skip_group_check=True).then_inc(ay_done, 1)

            run_steps(pe, 2, 0, step0)

            def turn_x(n, g):
                wait(pe, lo_done[n], g.count())
                wait(pe, xt_done[n], g.count(2))
                for h, part in enumerate((hi, lo)):
                    for c in range(C):
                        at = (2 * h + c) * P
                        t = nc.tensor.transpose(bank16[g.ring(2)][:, at:at + P],
                                                part[:, g.ring(4), c * P:(c + 1) * P], ident16[:])
                t.then_inc(trx_done[n], 1)

            def times_x(dst, g, w, a, b, first):
                for c in range(C):
                    m = split_product(dst, lambda h: xt[:, g.ring(8), 2 * h + c, :],
                                      lambda h: w[h][:, c, a:b], first and c == 0, c == C - 1)
                return m

            def step1(s):
                if g := s.item(0):
                    wait(pe, tlo_done, g.count())
                    wait(pe, tt_done, g.count(2))
                    for h in range(2):
                        t = nc.tensor.transpose(bank16[6 + g.ring(2)][:, h * P:(h + 1) * P],
                                                tr[:, g.ring(2), h, :], ident16[:])
                    t.then_inc(trt_done, 1)
                if g := s.item(3):
                    turn_x(1, g)
                if g := s.item(2):
                    b = bank[2 + g.ring(2)]
                    wait(pe, xt_done[1], g.count())
                    wait(pe, ylo_done, g.count(2))
                    times_x(b[:, 0:D + 2], g, w1, 2 * D, 3 * D + 2, True)
                    for c in range(C):
                        m = split_product(b[:, D + 2:D + 2 + P], lambda h: vj[h][:, c, :],
                                          lambda h: xt[:, g.ring(8), 2 * h + c, :], False, c == C - 1)
                    m.then_inc(xwb_done, 1)
                if g := s.item(0):
                    wait(pe, tt_done, g.count())
                    wait(pe, ylo_done, g.count())
                    split_product(bank[4 + g.ring(2)][:, D:2 * D], lambda h: tr_t[:, g.ring(2), h, :],
                                  lambda h: yh[:, g.ring(2), h, :], False).then_inc(ty_done, 1)
                if g := s.item(1):
                    b = bank[4 + g.ring(2)]
                    wait(pe, relu_done, g.count(2))
                    times_x(b[:], g, w1, 0, 2 * D, True)
                    nc.tensor.matmul(b[:, 0:D], ones1[:], bias1[:], start=False, stop=False,
                                     skip_group_check=True).then_inc(xwa_done, 1)
                if g := s.item(0):
                    wait(pe, zlo_done, g.count())
                    split_product(bank[4 + g.ring(2)][:, 0:D], lambda h: tr_t[:, g.ring(2), h, :],
                                  lambda h: zh[:, g.ring(2), h, :], False).then_inc(tz_done, 1)

            pe.wait_ge(alo_done, G)
            pe.wait_ge(res_done[0], G)
            run_steps(pe, 3, 0, step1)

            def gate_steps(n, s):
                if g := s.item(0):
                    b = bank[2 + g.ring(2)]
                    wait(pe, q_saved[n], g.count())
                    if n == 2:
                        split_product(b[:, D:2 * D], lambda h: am_t[:, g.index, h, :],
                                      lambda h: (hi, lo)[h][:, g.ring(4), :], False).then_inc(ax_done[2], 1)
                    else:
                        wait(pe, klo_done, g.count())
                        split_product(b[:, D:D + ATT], lambda h: an_t[:, g.index, h, :],
                                      lambda h: kh[:, g.ring(2), h, :], False).then_inc(ax_done[3], 1)
                if g := s.item(2):
                    turn_x(n, g)
                if g := s.item(1):
                    wait(pe, xt_done[n], g.count())
                    wait(pe, dot_done[n], g.count(2))
                    width = D if n == 2 else 2 * ATT
                    times_x(bank[2 + g.ring(2)][:, 0:width], g, w2 if n == 2 else w3, 0, width, True)\
                        .then_inc(qx_done[n], 1)
                if (g := s.item(-1)) and g.pos % QUAD == QUAD - 1:
                    wait(pe, logit_done[n], g.count())
                    wait(pe, pcol_done[n], g.count(4))
                    nc.tensor.matmul(bank[7][0:QUAD, 0:P], logits[:, g.ring(8) // QUAD, :], ident[:],
                                     start=True, stop=True).then_inc(turned[n], QUAD)
                if (g := s.item(-2)) and g.pos % QUAD == QUAD - 1:
                    wait(pe, prow_done[n], g.count())
                    nc.tensor.matmul(bank[7][:, P:P + QUAD], prow[:, g.ring(8) // QUAD, :],
                                     ident[0:QUAD, 0:QUAD], start=True, stop=True).then_inc(pback[n], QUAD)
                if g := s.item(1 - RES_LAG[n]):
                    wait(pe, res_done[n], g.count(2))
                    a = D if n == 2 else P
                    times_x(bank[4 + g.ring(2)][:, 0:D], g, w2 if n == 2 else w3, a, a + D, True)\
                        .then_inc(v_done[n], 1)

            pe.wait_ge(xt_done[1], G)
            pe.wait_ge(ylo_done, G)
            pe.wait_ge(relu_done, G)
            pe.wait_ge(tt_done, G)
            run_steps(pe, 2, RES_LAG[2] - 1, lambda s: gate_steps(2, s))
            pe.wait_ge(xt_done[2], G)
            pe.wait_ge(dot_done[2], G)
            pe.wait_ge(res_done[2], G)
            pe.wait_ge(pcol_done[2], G)
            run_steps(pe, 2, RES_LAG[3] - 1, lambda s: gate_steps(3, s))


_INPUTS = ["x", "adj", "nodemask", "L0_gnn_W", "L1_gnn_Wv", "L1_gnn_bv", "L1_gnn_aw", "L1_gnn_ab",
           "L1_gnn_Wk", "L1_gnn_bk", "L2_gnn_Wqk", "L2_gnn_Wv", "L3_gnn_W_qk", "L3_gnn_W_v"]


def kernel(**inputs):
    import numpy as np
    import concourse.bacc as bacc
    from concourse.bass_utils import run_bass_kernel_spmd

    nc = bacc.Bacc("TRN2", target_bir_lowering=False, num_devices=1)
    arrays, args = {}, []
    for name in _INPUTS:
        a = np.ascontiguousarray(inputs[name])
        if name == "L1_gnn_aw":
            a = a.reshape(-1)
        arrays[f"in_{name}"] = a
        args.append(nc.dram_tensor(f"in_{name}", a.shape, mybir.dt.from_np(a.dtype), kind="ExternalInput").ap())
    out = nc.dram_tensor("out_x", (G, P, D), F32, kind="ExternalOutput").ap()
    gnn_stack(nc, *args, out)
    result = run_bass_kernel_spmd(nc, [arrays], core_ids=[0])
    return result.results[0]["out_x"]
```

```python
from contextlib import ExitStack

import concourse.bass as bass
from concourse import mybir

F32 = mybir.dt.float32
F16 = mybir.dt.float16
ALU = mybir.AluOpType
ACT = mybir.ActivationFunctionType
AX_X = mybir.AxisListType.X

P = 128
G = 64
D = 256
C = D // P
ATT = 64
U = 8
QUAD = 4
SCALE = 64.0
PROD = SCALE * SCALE
DEG_EPS = 1e-6
ROW_EPS = 1e-12
LN_EPS = 1e-5
SLOPE = 0.2


N_LOADS = 12
BIAS_STEP = 7
PREP_ACT = 14
PREP_DVE = 28
QUEUE = 2


class Item:

    def __init__(self, index, pos):
        self.index, self.pos = index, pos

    def ring(self, depth):
        return self.pos % depth

    def count(self, back=0):
        return self.index + (1 - back)


class Step:
    def __init__(self, index, pos):
        self.index, self.pos = index, pos

    def item(self, offset):
        if isinstance(self.index, int) and not 0 <= self.index + offset < G:
            return None
        return Item(self.index + offset, (self.pos + offset) % U)

    def at(self, index):
        return isinstance(self.index, int) and self.index == index


def run_layers(eng, layers):
    before, before_lag = None, 0
    for n, (lead, lag, body, peel) in enumerate(layers):
        first = max(peel, -(-max(lag, before_lag) // U))
        for t in range(-lead, first * U):
            if before and t < before_lag:
                before(Step(G + t, t % U))
            body(Step(t, t % U))
        with eng.Fori(first, G // U - 1) as o:
            for v in range(U):
                body(Step(o * U + v, v))
        next_lead = layers[n + 1][0] if n + 1 < len(layers) else -lag
        for t in range(G - U, G - next_lead):
            body(Step(t, t % U))
        before, before_lag = body, lag


def wait(eng, sem, count):
    if isinstance(count, int) and count <= 0:
        return
    eng.wait_ge(sem, count)


def wait_back(eng, sem, g, back, layer_before=None):
    if not isinstance(g.index, int) or g.index >= back:
        eng.wait_ge(sem, g.count(back))
    elif layer_before is not None:
        eng.wait_ge(layer_before, G + g.count(back))


def gnn_stack(nc, x_in, adj_in, mask_in, w0_in, wv1_in, bv1_in, aw1_in, ab1_in, wk1_in, bk1_in,
              wqk2_in, wv2_in, wqk3_in, wv3_in, out):
    with ExitStack() as ctx:
        def sb(name, shape, dt=F32):
            return ctx.enter_context(nc.sbuf_tensor(name, shape, dt))

        def sem(name):
            return ctx.enter_context(nc.semaphore(name))

        x = sb("x", [P, G, D])
        adj = sb("adj", [P, G, P])
        an_t = sb("an_t", [P, G, 2, P], F16)
        am_t = sb("am_t", [P, G, 2, P], F16)
        deg_m = sb("deg_m", [P, G])
        w0 = sb("w0", [P, C, 2 * D])
        w1 = [sb(f"w1_{h}", [P, C, 3 * D + 2], F16) for h in ("hi", "lo")]
        vj = [sb(f"vj_{h}", [P, C, P], F16) for h in ("hi", "lo")]
        bias1 = sb("bias1", [P, D], F16)
        ones1 = sb("ones1", [P, P], F16)
        w2 = [sb(f"w2_{h}", [P, C, 2 * D], F16) for h in ("hi", "lo")]
        w3 = [sb(f"w3_{h}", [P, C, 3 * P], F16) for h in ("hi", "lo")]
        mask_t = sb("mask_t", [P, G])
        logit_c = sb("logit_c", [P, G])
        logit_d = sb("logit_d", [P, G])
        score_c = sb("score_c", [P, 1])
        ident = sb("ident", [P, P])
        ident16 = sb("ident16", [P, P], F16)
        minus_half = sb("minus_half", [P, QUAD])

        stages = [t[:].rearrange("p g h n -> p (g h n)") for t in (am_t, an_t)]
        at_word = [0, P * G // 2]

        def staged(words, where=0):
            a = 2 * at_word[where]
            at_word[where] += words
            assert at_word[where] <= G * P
            return stages[where][:, a:a + 2 * words].bitcast(F32)

        w0_nat = staged(C * 2 * D).rearrange("p (c f) -> p c f", c=C)
        mask_nat = staged(P)
        assert at_word[0] <= 2 * U * P
        at_word[0] = 2 * U * P
        wk_f = staged(C * 3 * D).rearrange("p (c k f) -> p c k f", c=C, k=3)
        wv1_f = staged(C * D).rearrange("p (c f) -> p c f", c=C)
        wqk2_nat = staged(C * 2 * D).rearrange("p (c f) -> p c f", c=C)
        wqk2_t = staged(4 * D).rearrange("p (a d) -> p a d", a=4)
        w2_f = staged(C * 2 * D).rearrange("p (c f) -> p c f", c=C)
        wqk3_nat = staged(D)
        w3_f = staged(C * 3 * P).rearrange("p (c f) -> p c f", c=C)
        bcast = staged(4 * D, 1)
        wv3_nat = staged(C * D, 1).rearrange("p (c f) -> p c f", c=C)
        prod = staged(6 * D, 1).rearrange("p (k f) -> p k f", k=6)
        shared = sb("shared", [P, 2 * (P * 4 + (D + P) * 4 + D * 4)], F16)
        taken = [0, 0, 0]

        def ring_of(layer, shape, dt=F32):
            size = 2 // (1 if dt == F32 else 2)
            for n in shape:
                size *= n
            at = taken[layer]
            taken[layer] += size
            flat = shared[:, at:at + size]
            flat = flat.bitcast(F32) if dt == F32 else flat
            names = "abc"[:len(shape)]
            sizes = dict(zip(names[1:], shape[1:]))
            return flat.rearrange(f"p ({' '.join(names)}) -> p {' '.join(names)}", **sizes)

        an = ring_of(0, [4, P])
        xa = ring_of(0, [4, D + P])
        y0 = ring_of(0, [4, D])
        vcols = sb("vcols", [P, 2, C])
        bsum = sb("bsum", [P, 4])

        parts = sb("parts", [P, 2, 4, D], F16)
        hi, lo = parts[:, 0], parts[:, 1]
        x_fixed = parts[:].rearrange("p h r d -> p (h r d)").bitcast(F32).rearrange("p (r d) -> p r d", r=4)
        xt = sb("xt", [P, 8, 4, P], F16)
        xt_f = xt[:].rearrange("p r c n -> p (r c n)").bitcast(F32)
        rows = xt_f[0:1, 0:4 * D + 2]
        bk_rows = xt_f[0:1, 4 * D + 2:7 * D + 2]
        ones_row = sb("ones_row", [1, P])
        dg = sb("dg", [P, 2, QUAD])
        rdeg = sb("rdeg", [P, 2, QUAD])
        u = ring_of(1, [2, P])
        lk = ring_of(1, [2, P])
        ex = ring_of(1, [2, P])
        alpha = ring_of(1, [2, P])
        asum = sb("asum", [P, 2, 1])
        rsum = sb("rsum", [P, 2, 1])
        rinv = sb("rinv", [P, 2, 1])
        tr = ring_of(1, [2, 2, P], F16)
        tr_t = ring_of(1, [2, 2, P], F16)
        zh = ring_of(1, [2, 2, D], F16)
        yh = ring_of(1, [2, 2, D], F16)
        hr = ring_of(1, [2, D])
        kh = ring_of(2, [2, 2, ATT], F16)
        qs = ring_of(2, [2, ATT])
        dots = sb("dots", [P, 2, QUAD])
        logits = sb("logits", [P, 2, QUAD])
        pmax = sb("pmax", [QUAD, 2, 1])
        nmax = sb("nmax", [QUAD, 2, 1])
        pexp = ring_of(2, [2, P])[0:QUAD]
        psums = sb("psums", [QUAD, 2, 1])
        pinv = sb("pinv", [QUAD, 2, 1])
        prow = ring_of(2, [2, P])[0:QUAD]
        pcol = sb("pcol", [P, 2, QUAD])
        junk = ring_of(2, [2, D])
        assert taken[2] <= taken[1] - 2 * 2 * D

        bst = sb("bst", [P, 8, 6])
        mv = sb("mv", [P, 2, QUAD, 2])
        veps = sb("veps", [P, 2, QUAD])
        rstd = sb("rstd", [P, 2, QUAD])
        nb = sb("nb", [P, 2, QUAD])

        bank = [ctx.enter_context(nc.psum_tensor(f"bank{i}", [P, 512], F32)) for i in range(8)]
        bank16 = [b[:].bitcast(F16) for b in bank]

        x_loaded = [sem(f"x_loaded{i}") for i in range(QUEUE)]
        a_loaded = [sem(f"a_loaded{i}") for i in range(QUEUE)]
        w0_loaded = sem("w0_loaded")
        w_loaded = sem("w_loaded")
        stored = sem("stored")
        ident_ready = sem("ident_ready")
        pool_ready = sem("pool_ready")
        prep_pe = sem("prep_pe")
        prep_dve = sem("prep_dve")
        prep_act = sem("prep_act")

        deg_done = sem("deg_done")
        degm_done = sem("degm_done")
        rdeg_done = sem("rdeg_done")
        x_fixed_done = sem("x_fixed_done")
        an_done = sem("an_done")
        tr0_done = sem("tr0_done")
        xa_done = sem("xa_done")
        ahi_done = sem("ahi_done")
        alo_done = sem("alo_done")
        xw0_done = sem("xw0_done")
        y0_done = sem("y0_done")
        ay_done = sem("ay_done")

        coef_done = sem("coef_done")
        hi_done = [None] + [sem(f"hi_done{n}") for n in (1, 2, 3)]
        lo_done = [None] + [sem(f"lo_done{n}") for n in (1, 2, 3)]
        trx_done = [None] + [sem(f"trx_done{n}") for n in (1, 2, 3)]
        xt_done = [None] + [sem(f"xt_done{n}") for n in (1, 2, 3)]

        xwb_done = sem("xwb_done")
        xwa_done = sem("xwa_done")
        u_done = sem("u_done")
        lk_done = sem("lk_done")
        ex_done = sem("ex_done")
        alpha_done = sem("alpha_done")
        rsum_done = sem("rsum_done")
        rinv_done = sem("rinv_done")
        thi_done = sem("thi_done")
        tlo_done = sem("tlo_done")
        trt_done = sem("trt_done")
        tt_done = sem("tt_done")
        yhi_done = sem("yhi_done")
        ylo_done = sem("ylo_done")
        ty_done = sem("ty_done")
        zhi_done = sem("zhi_done")
        zlo_done = sem("zlo_done")
        tz_done = sem("tz_done")
        relu_done = sem("relu_done")

        qx_done = [None, None, sem("xm_done"), sem("qk_done")]
        ax_done = [None, None, sem("ax_done"), sem("ak_done")]
        q_saved = [None, None, sem("xm_saved"), sem("q_saved")]
        khi_done = sem("khi_done")
        klo_done = sem("klo_done")
        dot_done = [None, None, sem("dot_done2"), sem("dot_done3")]
        logit_done = [None, None, sem("logit_done2"), sem("logit_done3")]
        turned = [None, None, sem("turned2"), sem("turned3")]
        pmax_done = [None, None, sem("pmax_done2"), sem("pmax_done3")]
        nmax_done = [None, None, sem("nmax_done2"), sem("nmax_done3")]
        pexp_done = [None, None, sem("pexp_done2"), sem("pexp_done3")]
        pinv_done = [None, None, sem("pinv_done2"), sem("pinv_done3")]
        prow_done = [None, None, sem("prow_done2"), sem("prow_done3")]
        pback = [None, None, sem("pback2"), sem("pback3")]
        pcol_done = [None, None, sem("pcol_done2"), sem("pcol_done3")]
        v_done = [None, None, sem("v_done2"), sem("v_done3")]

        res_done = [sem(f"res_done{n}") for n in range(4)]
        stats_done = [sem(f"stats_done{n}") for n in range(4)]
        aggr_done = [sem(f"aggr_done{n}") for n in range(4)]
        veps_done = [sem(f"veps_done{n}") for n in range(4)]
        rstd_done = [sem(f"rstd_done{n}") for n in range(4)]
        nb_done = [sem(f"nb_done{n}") for n in range(4)]
        norm_done = [sem(f"norm_done{n}") for n in range(4)]
        norm_even = sem("norm_even")

        hi_last = [None, trx_done[1], ax_done[2], trx_done[3]]
        xt_last = [None, xwa_done, v_done[2], v_done[3]]
        RES_LAG = [1, 1, 7, 7]
        NORM_LAG = [r + 7 for r in RES_LAG]

        block = ctx.enter_context(nc.Block())

        @block.sync
        def _(sp):
            def load(q, i):
                sp.dma_start(adj[:, bass.ds(q * QUAD, QUAD), :],
                             adj_in[bass.ds(q * QUAD, QUAD)].rearrange("g n m -> n g m"))\
                    .then_inc(a_loaded[i], 16)
                sp.dma_start(x[:, bass.ds(q * QUAD, QUAD), :],
                             x_in[bass.ds(q * QUAD, QUAD)].rearrange("g n d -> n g d"))\
                    .then_inc(x_loaded[i], 16)

            for i in range(QUEUE):
                load(i, i)
            loads = [
                (rows[:, 0:2 * D], aw1_in.rearrange("(a n) -> a n", a=1)),
                (rows[:, 2 * D:3 * D], bv1_in.rearrange("(a n) -> a n", a=1)),
                (rows[:, 4 * D:4 * D + 1], ab1_in.rearrange("(a n) -> a n", a=1)),
                (bk_rows, bk1_in.rearrange("(a k) n -> a (k n)", a=1)),
                (wv1_f, wv1_in.rearrange("(c p) f -> p c f", p=P)),
                (wqk2_nat, wqk2_in.rearrange("(c p) f -> p c f", p=P)),
                (w2_f[:, :, D:2 * D], wv2_in.rearrange("(c p) f -> p c f", p=P)),
                (wqk3_nat, wqk3_in),
                (wv3_nat, wv3_in.rearrange("(c p) f -> p c f", p=P)),
            ] + [(wk_f[:, :, k, :], wk1_in[k].rearrange("(c p) f -> p c f", p=P)) for k in range(3)]
            for dst, src in loads:
                sp.dma_start(dst, src).then_inc(w_loaded, 16)
            assert len(loads) == N_LOADS
            with sp.Fori(1, G // QUAD // QUEUE) as r:
                for i in range(QUEUE):
                    sp.wait_ge(a_loaded[i], 16 * r)
                    sp.wait_ge(x_loaded[i], 16 * r)
                    load(r * QUEUE + i, i)
            with sp.Fori(0, G // 2) as h:
                sp.wait_ge(norm_done[3], 2 * h + 2)
                sp.wait_ge(norm_even, 2 * h + 2)
                sp.dma_start(out[bass.ds(h * 2, 2)].rearrange("g n d -> n g d"),
                             x[:, bass.ds(h * 2, 2), :]).then_inc(stored, 16)
            sp.wait_ge(stored, 16 * (G // 2))

        @block.gpsimd
        def _(pool):
            nc.gpsimd.memset(ident[:], 0.0).then_inc(ident_ready, 1)
            nc.gpsimd.memset(ident16[:], 0.0).then_inc(ident_ready, 1)
            pool.wait_ge(ident_ready, 2)
            for m in (ident, ident16):
                nc.gpsimd.affine_select(out=m[:], in_=m[:], compare_op=ALU.not_equal, fill=1.0, base=0,
                                        pattern=[[-1, P]], channel_multiplier=1).then_inc(ident_ready, 1)
            nc.gpsimd.memset(minus_half[:], -0.5).then_inc(pool_ready, 1)
            pool.wait_ge(pool_ready, 1)
            nc.gpsimd.tensor_tensor(rstd[:, 0, :], minus_half[:], minus_half[:], ALU.mult).then_inc(pool_ready, 1)
            pool.wait_ge(pool_ready, 2)

            def inverse_root(n, g):
                if g is None or g.pos % QUAD != QUAD - 1:
                    return
                r = g.ring(8) // QUAD
                wait(pool, veps_done[n], g.count())
                wait_back(pool, norm_done[n], g, 8, norm_done[n - 1] if n else None)
                if n == 3:
                    wait_back(pool, norm_even, g, 8)
                nc.gpsimd.tensor_tensor(rstd[:, r, :], veps[:, r, :], minus_half[:], ALU.pow)\
                    .then_inc(rstd_done[n], QUAD)

            def step0(s):
                if g := s.item(3):
                    if g.pos % QUAD == 0:
                        pool.wait_ge(x_loaded[g.pos // QUAD], (g.index - g.pos) * 2 + 16)
                    wait(pool, tr0_done, g.count(4))
                    nc.gpsimd.tensor_copy(x_fixed[:, g.ring(4), :], x[:, g.index, :])\
                        .then_inc(x_fixed_done, 1)
                inverse_root(0, s.item(-RES_LAG[0] - 1))

            def later_step(n, lead):
                def step(s):
                    if g := s.item(lead):
                        if n == 1 and isinstance(g.index, int) and g.index < 4:
                            pool.wait_ge(tr0_done, G - 1 + g.index // 2)
                        wait(pool, hi_done[n], g.count())
                        nc.gpsimd.tensor_tensor(lo[:, g.ring(4), :], x[:, g.index, :], hi[:, g.ring(4), :],
                                                ALU.subtract).then_inc(lo_done[n], 1)
                    inverse_root(n, s.item(-RES_LAG[n] - 1))
                return step

            run_layers(pool, [(3, RES_LAG[0] + 1, step0, 2), (4, RES_LAG[1] + 1, later_step(1, 4), 2),
                              (3, RES_LAG[2] + 1, later_step(2, 3), 2), (3, RES_LAG[3] + 1, later_step(3, 3), 2)])

        @block.scalar
        def _(act):
            act.dma_start(w0_nat, w0_in.rearrange("(c p) f -> p c f", p=P)).then_inc(w0_loaded, 16)
            act.dma_start(mask_nat[0:G, :], mask_in).then_inc(w0_loaded, 16)
            nc.scalar.preload_act_table(ACT.Exp)

            act.wait_ge(prep_pe, 1)
            nc.scalar.activation(w0[:, 0, :], bank[0][:], ACT.Copy).then_inc(prep_act, 1)
            nc.scalar.activation(w0[:, 1, :], bank[1][:], ACT.Copy).then_inc(prep_act, 1)
            nc.scalar.activation(mask_t[:], bank[7][:, 0:G], ACT.Copy).then_inc(prep_act, 1)
            act.wait_ge(prep_act, 3)

            def prepare(s):
                if s.at(3):
                    act.wait_ge(w_loaded, 16 * N_LOADS)
                    nc.scalar.activation(w1[0][:, :, 0:3 * D], wk_f.rearrange("p c k f -> p c (k f)"),
                                         ACT.Copy, scale=SCALE).then_inc(prep_act, 1)
                if s.at(4):
                    act.wait_ge(prep_pe, 2)
                    nc.scalar.activation(bcast[:, 0:2 * D], bank[6][:], ACT.Copy).then_inc(prep_act, 1)
                if s.at(5):
                    act.wait_ge(prep_pe, 3)
                    nc.scalar.activation(bcast[:, 2 * D:4 * D], bank[7][:], ACT.Copy).then_inc(prep_act, 1)
                if s.at(6):
                    act.wait_ge(prep_pe, 4)
                    nc.scalar.activation(bsum[:, 3:4], bank[6][:, 0:1], ACT.Copy).then_inc(prep_act, 1)
                if s.at(7):
                    act.wait_ge(prep_pe, 5)
                    nc.scalar.activation(wqk2_t[:, 0:2, :].rearrange("p a d -> p (a d)"), bank[7][:],
                                         ACT.Copy).then_inc(prep_act, 1)
                if s.at(8):
                    act.wait_ge(prep_pe, 6)
                    nc.scalar.activation(wqk2_t[:, 2:4, :].rearrange("p a d -> p (a d)"), bank[6][:],
                                         ACT.Copy).then_inc(prep_act, 1)
                if s.at(9):
                    act.wait_ge(prep_pe, 7)
                    nc.scalar.activation(w3_f[:, :, P:3 * P], bank[7][:].rearrange("p (c e) -> p c e", c=C),
                                         ACT.Copy).then_inc(prep_act, 1)
                if s.at(10):
                    act.wait_ge(prep_pe, 8)
                    nc.scalar.activation(w3_f[:, :, 0:P], bank[6][:, 0:C * P].rearrange("p (c e) -> p c e", c=C),
                                         ACT.Copy).then_inc(prep_act, 1)
                    act.wait_ge(prep_act, 11)
                    nc.scalar.activation(w3[0][:], w3_f, ACT.Copy, scale=SCALE).then_inc(prep_act, 1)
                if s.at(11):
                    act.wait_ge(prep_pe, 9)
                    nc.scalar.activation(w2_f[:, :, 0:D], bank[7][:].rearrange("p (c e) -> p c e", c=C),
                                         ACT.Copy).then_inc(prep_act, 1)
                    act.wait_ge(prep_act, 13)
                    nc.scalar.activation(w2[0][:], w2_f, ACT.Copy, scale=SCALE).then_inc(prep_act, 1)
                if s.at(14):
                    act.wait_ge(prep_act, PREP_ACT)
                    act.wait_ge(prep_dve, PREP_DVE)

            def step0(s):
                prepare(s)
                if g := s.item(2):
                    wait(act, tr0_done, g.count())
                    wait(act, ay_done, g.count(4))
                    nc.scalar.activation(xa[:, g.ring(4), :], bank[g.ring(2)][:, 0:D + P], ACT.Copy)\
                        .then_inc(xa_done, 1)
                    nc.scalar.activation(an_t[:, g.index, 0, :], bank[g.ring(2)][:, D:D + P], ACT.Copy)
                    nc.scalar.activation(am_t[:, g.index, 0, :], bank[g.ring(2)][:, D:D + P], ACT.Copy,
                                         scale=mask_t[:, bass.ds(g.index, 1)]).then_inc(ahi_done, 1)
                if g := s.item(0):
                    wait(act, xw0_done, g.count())
                    nc.scalar.activation(y0[:, g.ring(4), :], bank[2 + g.ring(4)][:, D:2 * D], ACT.Copy,
                                         scale=1.0 / SCALE).then_inc(y0_done, 1)

            def split_hi(n, g):
                wait(act, norm_done[n - 1], g.count())
                if n == 1 and isinstance(g.index, int) and g.index < 4:
                    act.wait_ge(tr0_done, G - 3 + g.index // 2)
                wait_back(act, hi_last[n], g, 4, hi_last[n - 1])
                nc.scalar.activation(hi[:, g.ring(4), :], x[:, g.index, :], ACT.Copy).then_inc(hi_done[n], 1)

            def save_xt(n, g, last_reader, depth=8):
                wait(act, trx_done[n], g.count())
                wait_back(act, last_reader[n], g, depth, last_reader[n - 1])
                nc.scalar.activation(xt[:, g.ring(8), :, :].rearrange("p c n -> p (c n)"),
                                     bank16[g.ring(2)][:, 0:4 * P], ACT.Copy).then_inc(xt_done[n], 1)

            def step1(s):
                if g := s.item(-1):
                    wait(act, tz_done, g.count())
                    wait(act, res_done[1], g.count(2))
                    nc.scalar.activation(hr[:, g.ring(2), :], bank[4 + g.ring(2)][:, 0:D], ACT.Relu,
                                         scale=1.0 / SCALE).then_inc(relu_done, 1)
                if g := s.item(0):
                    wait(act, trt_done, g.count())
                    wait(act, tz_done, g.count(2))
                    nc.scalar.activation(tr_t[:, g.ring(2), :, :].rearrange("p h n -> p (h n)"),
                                         bank16[6 + g.ring(2)][:, 0:2 * P], ACT.Copy).then_inc(tt_done, 1)
                if g := s.item(3):
                    save_xt(1, g, xt_last)
                if g := s.item(4):
                    split_hi(1, g)
                if g := s.item(0):
                    wait(act, ty_done, g.count())
                    nc.scalar.activation(zh[:, g.ring(2), 0, :], bank[4 + g.ring(2)][:, D:2 * D], ACT.Copy,
                                         scale=1.0 / SCALE).then_inc(zhi_done, 1)
                if g := s.item(2):
                    wait(act, u_done, g.count())
                    wait(act, ty_done, g.count(2))
                    nc.scalar.activation(yh[:, g.ring(2), 0, :], bank[2 + g.ring(2)][:, 0:D], ACT.Copy,
                                         scale=1.0 / SCALE).then_inc(yhi_done, 1)
                    wait(act, lk_done, g.count())
                    wait(act, alpha_done, g.count(2))
                    nc.scalar.activation(ex[:, g.ring(2), :], lk[:, g.ring(2), :], ACT.Exp,
                                         scale=1.0 / PROD).then_inc(ex_done, 1)

            def softmax_exp(n, g):
                r = g.ring(8) // QUAD
                wait(act, nmax_done[n], g.count())
                wait_back(act, pback[n], g, 8, pback[n - 1])
                nc.scalar.activation(pexp[:, r, :], bank[7][0:QUAD, 0:P], ACT.Exp, bias=nmax[:, r, :],
                                     accum_out=psums[:, r, :]).then_inc(pexp_done[n], QUAD)

            def step2(s):
                if g := s.item(3):
                    split_hi(2, g)
                if g := s.item(1):
                    wait(act, qx_done[2], g.count())
                    wait_back(act, dot_done[2], g, 2, res_done[1])
                    nc.scalar.activation(hr[:, g.ring(2), :], bank[2 + g.ring(2)][:, 0:D], ACT.Copy)\
                        .then_inc(q_saved[2], 1)
                if (g := s.item(-2)) and g.pos % QUAD == QUAD - 1:
                    softmax_exp(2, g)
                if g := s.item(2):
                    save_xt(2, g, xt_last)

            def step3(s):
                if g := s.item(3):
                    split_hi(3, g)
                if (g := s.item(-NORM_LAG[3])) and g.pos % 2 == 0:
                    r, k = g.ring(8) // QUAD, g.ring(QUAD)
                    wait(act, nb_done[3], g.count(-(QUAD - 1 - k)))
                    nc.scalar.activation(x[:, g.index, :], x[:, g.index, :], ACT.Identity,
                                         bias=nb[:, r, k:k + 1], scale=rstd[:, r, k:k + 1])\
                        .then_inc(norm_even, 2)
                if g := s.item(1):
                    wait(act, qx_done[3], g.count())
                    wait(act, dot_done[3], g.count(2))
                    nc.scalar.activation(qs[:, g.ring(2), :], bank[2 + g.ring(2)][:, 0:ATT], ACT.Copy)\
                        .then_inc(q_saved[3], 1)
                    nc.scalar.activation(kh[:, g.ring(2), 0, :], bank[2 + g.ring(2)][:, ATT:2 * ATT], ACT.Copy,
                                         scale=1.0 / SCALE).then_inc(khi_done, 1)
                if (g := s.item(-2)) and g.pos % QUAD == QUAD - 1:
                    softmax_exp(3, g)
                if g := s.item(2):
                    save_xt(3, g, xt_last)

            run_layers(act, [(2, 0, step0, 2), (4, 1, step1, 1), (3, 2, step2, 2), (3, NORM_LAG[3], step3, 2)])

        @block.vector
        def _(dve):
            v = nc.vector
            v.memset(ones1[:], 1.0).then_inc(prep_dve, 1)
            v.memset(ones_row[:], 1.0).then_inc(prep_dve, 1)
            v.memset(rows[:, 4 * D + 1:4 * D + 2], 0.0).then_inc(prep_dve, 1)
            for w in w1:
                v.memset(w[:, :, 3 * D:3 * D + 2], 0.0).then_inc(prep_dve, 1)

            def prepare(s):
                if s.at(3):
                    dve.wait_ge(w_loaded, 16 * N_LOADS)
                    v.tensor_tensor(bk_rows[:, 0:D], bk_rows[:, 0:D], bk_rows[:, D:2 * D], ALU.add)\
                        .then_inc(prep_dve, 1)
                    dve.wait_ge(prep_dve, 6)
                    v.tensor_tensor(rows[:, 3 * D:4 * D], bk_rows[:, 0:D], bk_rows[:, 2 * D:3 * D], ALU.add)\
                        .then_inc(prep_dve, 1)
                for c in range(C):
                    if s.at(5 + c):
                        dve.wait_ge(prep_act, 4)
                        v.scalar_tensor_tensor(out=w1[1][:, c, 0:3 * D],
                                               in0=wk_f[:, c].rearrange("p k f -> p (k f)"), scalar=SCALE,
                                               in1=w1[0][:, c, 0:3 * D], op0=ALU.mult, op1=ALU.subtract)\
                            .then_inc(prep_dve, 1)
                for j in range(2):
                    if s.at(7 + j):
                        dve.wait_ge(prep_act, 7)
                        for c in range(C):
                            v.scalar_tensor_tensor(out=prod[:, 3 * j + c, :], in0=wv1_f[:, c, :], scalar=SCALE,
                                                   in1=bcast[:, j * D:(j + 1) * D], op0=ALU.mult, op1=ALU.mult,
                                                   accum_out=vcols[:, j, c:c + 1]).then_inc(prep_dve, 1)
                        v.scalar_tensor_tensor(out=prod[:, 3 * j + 2, :], in0=bcast[:, 2 * D:3 * D], scalar=1.0,
                                               in1=bcast[:, j * D:(j + 1) * D], op0=ALU.mult, op1=ALU.mult,
                                               accum_out=bsum[:, j:j + 1]).then_inc(prep_dve, 1)
                if s.at(9):
                    dve.wait_ge(prep_dve, 15)
                    v.tensor_tensor(bsum[:, 2:3], bsum[:, 0:1], bsum[:, 1:2], ALU.add).then_inc(prep_dve, 1)
                    v.tensor_copy(w1[0][:, :, 3 * D], vcols[:, 1, :]).then_inc(prep_dve, 1)
                    dve.wait_ge(prep_dve, 17)
                    v.tensor_scalar(score_c[:], bsum[:, 2:3], bsum[:, 3:4], PROD, ALU.add, ALU.mult)\
                        .then_inc(prep_dve, 1)
                    v.tensor_tensor(w1[1][:, :, 3 * D], vcols[:, 1, :], w1[0][:, :, 3 * D], ALU.subtract)\
                        .then_inc(prep_dve, 1)
                if s.at(10):
                    for c in range(C):
                        v.tensor_scalar(vj[0][:, c, :], ones1[:], vcols[:, 0, c:c + 1], None, ALU.mult)\
                            .then_inc(prep_dve, 1)
                    dve.wait_ge(prep_dve, 21)
                    for c in range(C):
                        v.scalar_tensor_tensor(out=vj[1][:, c, :], in0=ones1[:], scalar=vcols[:, 0, c:c + 1],
                                               in1=vj[0][:, c, :], op0=ALU.mult, op1=ALU.subtract)\
                            .then_inc(prep_dve, 1)
                if s.at(11):
                    v.tensor_scalar(bias1[:], bcast[:, 3 * D:4 * D], SCALE, None, ALU.mult)\
                        .then_inc(prep_dve, 1)
                    dve.wait_ge(prep_dve, 24)
                    v.tensor_copy(prod[P // 2:P, 0, :], bias1[P // 2:P, :]).then_inc(prep_dve, 1)
                    dve.wait_ge(prep_dve, 25)
                    v.scalar_tensor_tensor(out=bias1[P // 2:P, :], in0=bcast[P // 2:P, 3 * D:4 * D],
                                           scalar=SCALE, in1=prod[P // 2:P, 0, :], op0=ALU.mult,
                                           op1=ALU.subtract).then_inc(prep_dve, 1)
                if s.at(12):
                    dve.wait_ge(prep_act, 12)
                    v.scalar_tensor_tensor(out=w3[1][:], in0=w3_f, scalar=SCALE, in1=w3[0][:],
                                           op0=ALU.mult, op1=ALU.subtract).then_inc(prep_dve, 1)
                if s.at(13):
                    dve.wait_ge(prep_act, PREP_ACT)
                    v.scalar_tensor_tensor(out=w2[1][:], in0=w2_f, scalar=SCALE, in1=w2[0][:],
                                           op0=ALU.mult, op1=ALU.subtract).then_inc(prep_dve, 1)
                    dve.wait_ge(prep_dve, PREP_DVE)

            def norm_stats(n, s):
                if g := s.item(-RES_LAG[n]):
                    dve.wait_ge(prep_dve, 1)
                    wait(dve, res_done[n], g.count())
                    v.bn_stats(bst[:, g.ring(8), :], x[:, g.index, :]).then_inc(stats_done[n], 1)

            def norm_aggr(n, s):
                if g := s.item(-RES_LAG[n] - 1):
                    dve.wait_ge(prep_dve, 1)
                    wait(dve, stats_done[n], g.count())
                    v.bn_aggr(mv[:, g.ring(8) // QUAD, g.ring(QUAD), :], bst[:, g.ring(8), :])\
                        .then_inc(aggr_done[n], 1)

            def norm_veps(n, s):
                scale2 = 1.0 if n == 0 else PROD
                to = 1.0 / PROD if n < 3 else 1.0
                if (g := s.item(-RES_LAG[n] - 1)) and g.pos % QUAD == QUAD - 1:
                    r = g.ring(8) // QUAD
                    wait(dve, aggr_done[n], g.count())
                    v.tensor_scalar(veps[:, r, :], mv[:, r, :, 1], scale2 * LN_EPS, to, ALU.add, ALU.mult)\
                        .then_inc(veps_done[n], QUAD)

            def norm_apply(n, s):
                if (g := s.item(-NORM_LAG[n])) and (n < 3 or g.pos % 2):
                    r, k = g.ring(8) // QUAD, g.ring(QUAD)
                    wait(dve, nb_done[n], g.count(-(QUAD - 1 - k)))
                    v.tensor_scalar(x[:, g.index, :], x[:, g.index, :], rstd[:, r, k:k + 1],
                                    nb[:, r, k:k + 1], ALU.mult, ALU.add).then_inc(norm_done[n], 2 if n == 3 else 1)
                if (g := s.item(-RES_LAG[n] - 3)) and g.pos % QUAD == QUAD - 1:
                    r = g.ring(8) // QUAD
                    wait(dve, rstd_done[n], g.count())
                    v.scalar_tensor_tensor(out=nb[:, r, :], in0=mv[:, r, :, 0], scalar=-1.0,
                                           in1=rstd[:, r, :], op0=ALU.mult, op1=ALU.mult)\
                        .then_inc(nb_done[n], QUAD)

            def step0(s):
                prepare(s)
                quad = (g := s.item(4)) and g.pos % QUAD == 0 and g
                if g := quad:
                    r = g.pos // QUAD
                    dve.wait_ge(a_loaded[r], (g.index - g.pos) * 2 + 16)
                    v.tensor_reduce(dg[:, r, :], adj[:, bass.ds(g.index, QUAD), :], AX_X, ALU.add)\
                        .then_inc(deg_done, QUAD)
                if g := s.item(-1):
                    wait(dve, ay_done, g.count())
                    v.scalar_tensor_tensor(out=x[:, g.index, :], in0=bank[2 + g.ring(4)][:, 0:D], scalar=0.0,
                                           in1=x[:, g.index, :], op0=ALU.max, op1=ALU.add)\
                        .then_inc(res_done[0], 1)
                if g := quad:
                    wait(dve, deg_done, g.count(1 - QUAD))
                    v.tensor_scalar(deg_m[:, bass.ds(g.index, QUAD)], dg[:, g.pos // QUAD, :], DEG_EPS, None,
                                    ALU.max).then_inc(degm_done, QUAD)
                norm_aggr(0, s)
                norm_apply(0, s)
                if g := quad:
                    wait(dve, degm_done, g.count(1 - QUAD))
                    v.reciprocal(rdeg[:, g.pos // QUAD, :], deg_m[:, bass.ds(g.index, QUAD)])\
                        .then_inc(rdeg_done, QUAD)
                norm_stats(0, s)
                norm_veps(0, s)
                if g := s.item(3):
                    r, k = g.pos // QUAD, g.pos % QUAD
                    wait(dve, rdeg_done, g.count(k + 1 - QUAD))
                    wait(dve, tr0_done, g.count(4))
                    v.tensor_scalar(an[:, g.ring(4), :], adj[:, g.index, :], rdeg[:, r, k:k + 1], SCALE,
                                    ALU.mult, ALU.mult).then_inc(an_done, 1)
                if g := s.item(2):
                    wait(dve, ahi_done, g.count())
                    a_t = bank[g.ring(2)][:, D:D + P]
                    v.tensor_tensor(an_t[:, g.index, 1, :], a_t, an_t[:, g.index, 0, :], ALU.subtract)
                    v.scalar_tensor_tensor(out=am_t[:, g.index, 1, :], in0=a_t,
                                           scalar=mask_t[:, bass.ds(g.index, 1)], in1=am_t[:, g.index, 0, :],
                                           op0=ALU.mult, op1=ALU.subtract).then_inc(alo_done, 1)

            def step1(s):
                if s.pos == 0 and (g := s.item(-2)):
                    wait(dve, res_done[1], g.count())
                norm_apply(1, s)
                norm_aggr(1, s)
                if g := s.item(1):
                    r = g.ring(2)
                    wait(dve, ex_done, g.count())
                    v.scalar_tensor_tensor(out=alpha[:, r, :], in0=adj[:, g.index, :], scalar=1.0,
                                           in1=ex[:, r, :], op0=ALU.mult, op1=ALU.mult,
                                           accum_out=asum[:, r, :]).then_inc(alpha_done, 1)
                norm_veps(1, s)
                if g := s.item(1):
                    wait(dve, yhi_done, g.count())
                    v.scalar_tensor_tensor(out=yh[:, r, 1, :], in0=bank[2 + r][:, 0:D], scalar=1.0 / SCALE,
                                           in1=yh[:, r, 0, :], op0=ALU.mult, op1=ALU.subtract)\
                        .then_inc(ylo_done, 1)
                    wait(dve, alpha_done, g.count())
                    v.tensor_scalar(rsum[:, r, :], asum[:, r, :], ROW_EPS, 1.0 / SCALE, ALU.add, ALU.mult)\
                        .then_inc(rsum_done, 1)
                if g := s.item(-1):
                    wait(dve, relu_done, g.count())
                    v.tensor_tensor(x[:, g.index, :], x[:, g.index, :], hr[:, g.ring(2), :], ALU.add)\
                        .then_inc(res_done[1], 1)
                if g := s.item(1):
                    r = g.ring(2)
                    wait(dve, rsum_done, g.count())
                    v.reciprocal(rinv[:, r, :], rsum[:, r, :]).then_inc(rinv_done, 1)
                    wait(dve, rinv_done, g.count())
                    v.tensor_scalar(tr[:, r, 0, :], alpha[:, r, :], rinv[:, r, :], None, ALU.mult)\
                        .then_inc(thi_done, 1)
                if g := s.item(2):
                    xwb = bank[2 + g.ring(2)]
                    wait(dve, xwb_done, g.count())
                    v.tensor_scalar(u[:, g.ring(2), :], xwb[:, D + 2:D + 2 + P], xwb[:, D:D + 1],
                                    score_c[:, 0:1], ALU.add, ALU.add).then_inc(u_done, 1)
                if g := s.item(1):
                    r = g.ring(2)
                    wait(dve, thi_done, g.count())
                    v.scalar_tensor_tensor(out=tr[:, r, 1, :], in0=alpha[:, r, :], scalar=rinv[:, r, :],
                                           in1=tr[:, r, 0, :], op0=ALU.mult, op1=ALU.subtract)\
                        .then_inc(tlo_done, 1)
                if g := s.item(2):
                    wait(dve, u_done, g.count())
                    v.scalar_tensor_tensor(out=lk[:, g.ring(2), :], in0=u[:, g.ring(2), :], scalar=SLOPE,
                                           in1=u[:, g.ring(2), :], op0=ALU.mult, op1=ALU.max)\
                        .then_inc(lk_done, 1)
                if g := s.item(0):
                    wait(dve, zhi_done, g.count())
                    v.scalar_tensor_tensor(out=zh[:, g.ring(2), 1, :], in0=bank[4 + g.ring(2)][:, D:2 * D],
                                           scalar=1.0 / SCALE, in1=zh[:, g.ring(2), 0, :],
                                           op0=ALU.mult, op1=ALU.subtract).then_inc(zlo_done, 1)
                norm_stats(1, s)
                if s.at(7):
                    v.tensor_scalar(logit_d[:], deg_m[:], 1.0 / (8 * PROD * PROD), None, ALU.mult)\
                        .then_inc(coef_done, 1)
                    v.scalar_tensor_tensor(out=logit_c[:], in0=deg_m[:], scalar=1.0 / (16 * PROD * PROD),
                                           in1=mask_t[:], op0=ALU.mult, op1=ALU.mult).then_inc(coef_done, 1)
                    dve.wait_ge(coef_done, 2)

            def gate_steps(n, width, s):
                quad2 = (g := s.item(-2)) and g.pos % QUAD == QUAD - 1 and g
                quad3 = (g := s.item(-3)) and g.pos % QUAD == QUAD - 1 and g
                quad4 = (g := s.item(-4)) and g.pos % QUAD == QUAD - 1 and g
                if n == 3 and (g := s.item(0)):
                    wait(dve, khi_done, g.count())
                    v.scalar_tensor_tensor(out=kh[:, g.ring(2), 1, :], in0=bank[2 + g.ring(2)][:, ATT:2 * ATT],
                                           scalar=1.0 / SCALE, in1=kh[:, g.ring(2), 0, :],
                                           op0=ALU.mult, op1=ALU.subtract).then_inc(klo_done, 1)
                if g := quad2:
                    wait(dve, turned[n], g.count())
                    v.tensor_reduce(pmax[:, g.ring(8) // QUAD, :], bank[7][0:QUAD, 0:P], AX_X, ALU.max)\
                        .then_inc(pmax_done[n], QUAD)
                if g := quad4:
                    wait(dve, pback[n], g.count())
                    v.tensor_copy(pcol[:, g.ring(8) // QUAD, :], bank[7][:, P:P + QUAD])\
                        .then_inc(pcol_done[n], QUAD)
                norm_apply(n, s)
                if g := quad2:
                    r = g.ring(8) // QUAD
                    wait(dve, pmax_done[n], g.count())
                    v.tensor_scalar(nmax[:, r, :], pmax[:, r, :], -1.0, None, ALU.mult)\
                        .then_inc(nmax_done[n], QUAD)
                if g := quad3:
                    r = g.ring(8) // QUAD
                    wait(dve, pexp_done[n], g.count())
                    v.reciprocal(pinv[:, r, :], psums[:, r, :]).then_inc(pinv_done[n], QUAD)
                if g := s.item(-RES_LAG[n]):
                    r, k = g.ring(8) // QUAD, g.ring(QUAD)
                    wait(dve, v_done[n], g.count())
                    wait(dve, pcol_done[n], g.count(k + 1 - QUAD))
                    v.scalar_tensor_tensor(out=x[:, g.index, :], in0=bank[4 + g.ring(2)][:, 0:D],
                                           scalar=pcol[:, r, k:k + 1], in1=x[:, g.index, :],
                                           op0=ALU.mult, op1=ALU.add).then_inc(res_done[n], 1)
                if g := quad3:
                    r = g.ring(8) // QUAD
                    wait(dve, pinv_done[n], g.count())
                    v.tensor_scalar(prow[:, r, :], pexp[:, r, :], pinv[:, r, :], 1.0 / SCALE,
                                    ALU.mult, ALU.mult).then_inc(prow_done[n], QUAD)
                if s.pos == 0 and (g := s.item(-RES_LAG[n] - 1)):
                    wait(dve, res_done[n], g.count())
                if g := s.item(0):
                    r, k = g.ring(8) // QUAD, g.ring(QUAD)
                    wait(dve, ax_done[n], g.count())
                    wait(dve, q_saved[n], g.count())
                    v.scalar_tensor_tensor(out=junk[:, g.ring(2), 0:width],
                                           in0=bank[2 + g.ring(2)][:, D:D + width], scalar=1.0,
                                           in1=(hr if n == 2 else qs)[:, g.ring(2), :],
                                           op0=ALU.mult, op1=ALU.mult, accum_out=dots[:, r, k:k + 1])\
                        .then_inc(dot_done[n], 1)
                norm_aggr(n, s)
                norm_stats(n, s)
                norm_veps(n, s)
                if (g := s.item(0)) and g.pos % QUAD == QUAD - 1:
                    r = g.ring(8) // QUAD
                    wait(dve, dot_done[n], g.count())
                    v.tensor_tensor(logits[:, r, :], dots[:, r, :],
                                    (logit_c if n == 2 else logit_d)[:, bass.ds(g.index - (QUAD - 1), QUAD)],
                                    ALU.mult).then_inc(logit_done[n], QUAD)

            run_layers(dve, [(4, NORM_LAG[0], step0, 2), (2, NORM_LAG[1], step1, 1),
                             (0, NORM_LAG[2], lambda s: gate_steps(2, D, s), 1),
                             (0, NORM_LAG[3], lambda s: gate_steps(3, ATT, s), 1)])

        @block.tensor
        def _(pe):
            pe.wait_ge(ident_ready, 4)
            pe.wait_ge(w0_loaded, 32)

            for c in range(C):
                for half in range(2):
                    for o in range(2):
                        at = half * D + o * P
                        nc.tensor.transpose(bank[c][:, at:at + P],
                                            w0_nat[:, o, half * D + c * P:half * D + (c + 1) * P], ident[:])
            nc.tensor.transpose(bank[7][:, 0:G], mask_nat[0:G, :], ident[0:G, 0:G]).then_inc(prep_pe, 1)
            pe.wait_ge(prep_act, 3)

            def prepare(s):
                if s.at(3):
                    pe.wait_ge(w_loaded, 16 * N_LOADS)
                    pe.wait_ge(prep_dve, 5)
                    nc.tensor.matmul(bank[6][:], ones_row[:], rows[:, 0:2 * D], start=True, stop=True)\
                        .then_inc(prep_pe, 1)
                if s.at(4):
                    pe.wait_ge(prep_dve, BIAS_STEP)
                    nc.tensor.matmul(bank[7][:], ones_row[:], rows[:, 2 * D:4 * D], start=True, stop=True)\
                        .then_inc(prep_pe, 1)
                if s.at(5):
                    pe.wait_ge(prep_act, 5)
                    nc.tensor.matmul(bank[6][:, 0:2], ones_row[:], rows[:, 4 * D:4 * D + 2], start=True,
                                     stop=True).then_inc(prep_pe, 1)
                for half in range(2):
                    if s.at(6 + half):
                        pe.wait_ge(prep_act, 6 + half)
                        for a in range(2):
                            for c in range(C):
                                at = a * D + c * P
                                t = nc.tensor.transpose(bank[7 - half][:, at:at + P],
                                                        wqk2_nat[:, c, half * D + a * P:half * D + (a + 1) * P],
                                                        ident[:])
                        t.then_inc(prep_pe, 1)
                if s.at(8):
                    pe.wait_ge(prep_act, 8)
                    for c in range(C):
                        for o in range(2):
                            at = c * D + o * P
                            t = nc.tensor.transpose(bank[7][:, at:at + P], wv3_nat[:, o, c * P:(c + 1) * P],
                                                    ident[:])
                    t.then_inc(prep_pe, 1)
                if s.at(9):
                    pe.wait_ge(prep_act, 9)
                    for c in range(C):
                        t = nc.tensor.transpose(bank[6][:, c * P:(c + 1) * P], wqk3_nat[:, c * P:(c + 1) * P],
                                                ident[:])
                    t.then_inc(prep_pe, 1)
                if s.at(10):
                    pe.wait_ge(prep_act, 10)
                    for c in range(C):
                        for a in range(2):
                            t = nc.tensor.matmul(bank[7][:, c * D:(c + 1) * D],
                                                 wqk2_t[:, a, c * P:(c + 1) * P], wqk2_t[:, 2 + a, :],
                                                 start=(c == 0 and a == 0), stop=(a == 1),
                                                 skip_group_check=True)
                    t.then_inc(prep_pe, 1)

            def split_product(dst, left, right, first, last=True):
                for n, (a, b) in enumerate(((0, 0), (0, 1), (1, 0))):
                    m = nc.tensor.matmul(dst, left(a), right(b), start=first and n == 0, stop=last and n == 2,
                                         skip_group_check=True)
                return m

            def step0(s):
                if g := s.item(2):
                    wait(pe, x_fixed_done, g.count())
                    wait(pe, an_done, g.count())
                    wait(pe, alo_done, g.count(2))
                    b = bank[g.ring(2)]
                    for c in range(C):
                        nc.tensor.transpose(b[:, c * P:(c + 1) * P], x_fixed[:, g.ring(4), c * P:(c + 1) * P],
                                            ident[:])
                    nc.tensor.transpose(b[:, D:D + P], an[:, g.ring(4), :], ident[:]).then_inc(tr0_done, 1)
                if g := s.item(1):
                    wait(pe, xa_done, g.count())
                    wait(pe, res_done[0], g.count(4))
                    for c in range(C):
                        m = nc.tensor.matmul(bank[2 + g.ring(4)][:], xa[:, g.ring(4), c * P:(c + 1) * P],
                                             w0[:, c, :], start=(c == 0), stop=False, skip_group_check=True)
                    m.then_inc(xw0_done, 1)
                if g := s.item(0):
                    wait(pe, y0_done, g.count())
                    nc.tensor.matmul(bank[2 + g.ring(4)][:, 0:D], xa[:, g.ring(4), D:D + P], y0[:, g.ring(4), :],
                                     start=False, stop=True, skip_group_check=True).then_inc(ay_done, 1)
                prepare(s)


            def turn_x(n, g):
                wait(pe, lo_done[n], g.count())
                wait_back(pe, xt_done[n], g, 2, alo_done if n == 1 else xt_done[n - 1])
                for h, part in enumerate((hi, lo)):
                    for c in range(C):
                        at = (2 * h + c) * P
                        t = nc.tensor.transpose(bank16[g.ring(2)][:, at:at + P],
                                                part[:, g.ring(4), c * P:(c + 1) * P], ident16[:])
                t.then_inc(trx_done[n], 1)

            def times_x(dst, g, w, a, b, first):
                for c in range(C):
                    m = split_product(dst, lambda h: xt[:, g.ring(8), 2 * h + c, :],
                                      lambda h: w[h][:, c, a:b], first and c == 0, c == C - 1)
                return m

            def step1(s):
                if g := s.item(0):
                    wait(pe, tlo_done, g.count())
                    wait(pe, tt_done, g.count(2))
                    for h in range(2):
                        t = nc.tensor.transpose(bank16[6 + g.ring(2)][:, h * P:(h + 1) * P],
                                                tr[:, g.ring(2), h, :], ident16[:])
                    t.then_inc(trt_done, 1)
                if s.at(-3):
                    pe.wait_ge(prep_act, PREP_ACT)
                    pe.wait_ge(prep_dve, PREP_DVE)
                if g := s.item(3):
                    turn_x(1, g)
                if g := s.item(2):
                    b = bank[2 + g.ring(2)]
                    wait(pe, xt_done[1], g.count())
                    if s.at(-2) or s.at(-1):
                        pe.wait_ge(res_done[0], G - 3 + g.index)
                    wait(pe, ylo_done, g.count(2))
                    times_x(b[:, 0:D + 2], g, w1, 2 * D, 3 * D + 2, True)
                    for c in range(C):
                        m = split_product(b[:, D + 2:D + 2 + P], lambda h: vj[h][:, c, :],
                                          lambda h: xt[:, g.ring(8), 2 * h + c, :], False, c == C - 1)
                    m.then_inc(xwb_done, 1)
                if g := s.item(0):
                    wait(pe, tt_done, g.count())
                    wait(pe, ylo_done, g.count())
                    split_product(bank[4 + g.ring(2)][:, D:2 * D], lambda h: tr_t[:, g.ring(2), h, :],
                                  lambda h: yh[:, g.ring(2), h, :], False).then_inc(ty_done, 1)
                if g := s.item(1):
                    b = bank[4 + g.ring(2)]
                    wait_back(pe, relu_done, g, 2, res_done[0])
                    times_x(b[:], g, w1, 0, 2 * D, True)
                    nc.tensor.matmul(b[:, 0:D], ones1[:], bias1[:], start=False, stop=False,
                                     skip_group_check=True).then_inc(xwa_done, 1)
                if g := s.item(0):
                    wait(pe, zlo_done, g.count())
                    split_product(bank[4 + g.ring(2)][:, 0:D], lambda h: tr_t[:, g.ring(2), h, :],
                                  lambda h: zh[:, g.ring(2), h, :], False).then_inc(tz_done, 1)

            def gate_steps(n, s):
                if (g := s.item(-4)) and g.pos % QUAD == QUAD - 1:
                    wait(pe, prow_done[n], g.count())
                    nc.tensor.matmul(bank[7][:, P:P + QUAD], prow[:, g.ring(8) // QUAD, :],
                                     ident[0:QUAD, 0:QUAD], start=True, stop=True).then_inc(pback[n], QUAD)
                if g := s.item(1 - RES_LAG[n]):
                    wait_back(pe, res_done[n], g, 2, relu_done if n == 2 else res_done[n - 1])
                    a = D if n == 2 else P
                    times_x(bank[4 + g.ring(2)][:, 0:D], g, w2 if n == 2 else w3, a, a + D, True)\
                        .then_inc(v_done[n], 1)
                if g := s.item(0):
                    b = bank[2 + g.ring(2)]
                    if n == 2:
                        wait(pe, q_saved[n], g.count())
                        split_product(b[:, D:2 * D], lambda h: am_t[:, g.index, h, :],
                                      lambda h: (hi, lo)[h][:, g.ring(4), :], False).then_inc(ax_done[2], 1)
                    else:
                        wait(pe, klo_done, g.count())
                        split_product(b[:, D:D + ATT], lambda h: an_t[:, g.index, h, :],
                                      lambda h: kh[:, g.ring(2), h, :], False).then_inc(ax_done[3], 1)
                if g := s.item(1):
                    wait(pe, xt_done[n], g.count())
                    wait_back(pe, dot_done[n], g, 2, ylo_done if n == 2 else dot_done[n - 1])
                    width = D if n == 2 else 2 * ATT
                    times_x(bank[2 + g.ring(2)][:, 0:width], g, w2 if n == 2 else w3, 0, width, True)\
                        .then_inc(qx_done[n], 1)
                if g := s.item(2):
                    turn_x(n, g)
                if (g := s.item(-1)) and g.pos % QUAD == QUAD - 1:
                    wait(pe, logit_done[n], g.count())
                    wait_back(pe, pcol_done[n], g, 4, tt_done if n == 2 else pcol_done[n - 1])
                    nc.tensor.matmul(bank[7][0:QUAD, 0:P], logits[:, g.ring(8) // QUAD, :], ident[:],
                                     start=True, stop=True).then_inc(turned[n], QUAD)

            run_layers(pe, [(2, 0, step0, 2), (3, 0, step1, 1),
                            (2, RES_LAG[2] - 1, lambda s: gate_steps(2, s), 1),
                            (2, RES_LAG[3] - 1, lambda s: gate_steps(3, s), 1)])


_INPUTS = ["x", "adj", "nodemask", "L0_gnn_W", "L1_gnn_Wv", "L1_gnn_bv", "L1_gnn_aw", "L1_gnn_ab",
           "L1_gnn_Wk", "L1_gnn_bk", "L2_gnn_Wqk", "L2_gnn_Wv", "L3_gnn_W_qk", "L3_gnn_W_v"]


def kernel(**inputs):
    import numpy as np
    import concourse.bacc as bacc
    from concourse.bass_utils import run_bass_kernel_spmd

    nc = bacc.Bacc("TRN2", target_bir_lowering=False, num_devices=1)
    arrays, args = {}, []
    for name in _INPUTS:
        a = np.ascontiguousarray(inputs[name])
        if name == "L1_gnn_aw":
            a = a.reshape(-1)
        arrays[f"in_{name}"] = a
        args.append(nc.dram_tensor(f"in_{name}", a.shape, mybir.dt.from_np(a.dtype), kind="ExternalInput").ap())
    out = nc.dram_tensor("out_x", (G, P, D), F32, kind="ExternalOutput").ap()
    gnn_stack(nc, *args, out)
    result = run_bass_kernel_spmd(nc, [arrays], core_ids=[0])
    return result.results[0]["out_x"]
```

```python
from contextlib import ExitStack

import concourse.bass as bass
from concourse import mybir

F32 = mybir.dt.float32
F16 = mybir.dt.float16
ALU = mybir.AluOpType
ACT = mybir.ActivationFunctionType
AX_X = mybir.AxisListType.X

P = 128
G = 64
D = 256
C = D // P
ATT = 64
U = 8
QUAD = 4
SCALE = 64.0
PROD = SCALE * SCALE
X_SCALE = 16.0
DEG_EPS = 1e-6
ROW_EPS = 1e-12
LN_EPS = 1e-5
SLOPE = 0.2

N_LOADS = 12
BIAS_STEP = 5
PREP_ACT = 14
PREP_DVE = 23
QUEUE = 2


class Item:

    def __init__(self, index, pos):
        self.index, self.pos = index, pos

    def ring(self, depth):
        return self.pos % depth

    def count(self, back=0):
        return self.index + (1 - back)


class Step:
    def __init__(self, index, pos):
        self.index, self.pos = index, pos

    def item(self, offset):
        if isinstance(self.index, int) and not 0 <= self.index + offset < G:
            return None
        return Item(self.index + offset, (self.pos + offset) % U)

    def at(self, index):
        return isinstance(self.index, int) and self.index == index


def run_layers(eng, layers):
    before, before_lag = None, 0
    for n, (lead, lag, body, peel) in enumerate(layers):
        first = max(peel, -(-max(lag, before_lag) // U))
        for t in range(-lead, first * U):
            if before and t < before_lag:
                before(Step(G + t, t % U))
            body(Step(t, t % U))
        with eng.Fori(first, G // U - 1) as o:
            for v in range(U):
                body(Step(o * U + v, v))
        next_lead = layers[n + 1][0] if n + 1 < len(layers) else -lag
        for t in range(G - U, G - next_lead):
            body(Step(t, t % U))
        before, before_lag = body, lag


def wait(eng, sem, count):
    if isinstance(count, int) and count <= 0:
        return
    eng.wait_ge(sem, count)


def wait_back(eng, sem, g, back, layer_before=None):
    if not isinstance(g.index, int) or g.index >= back:
        eng.wait_ge(sem, g.count(back))
    elif layer_before is not None:
        eng.wait_ge(layer_before, G + g.count(back))


def gnn_stack(nc, x_in, adj_in, mask_in, w0_in, wv1_in, bv1_in, aw1_in, ab1_in, wk1_in, bk1_in,
              wqk2_in, wv2_in, wqk3_in, wv3_in, out):
    with ExitStack() as ctx:
        def sb(name, shape, dt=F32):
            return ctx.enter_context(nc.sbuf_tensor(name, shape, dt))

        def sem(name):
            return ctx.enter_context(nc.semaphore(name))

        x = sb("x", [P, G, D])
        adj = sb("adj", [P, G, P])
        an_t = sb("an_t", [P, G, 2, P], F16)
        am_t = sb("am_t", [P, G, 2, P], F16)
        deg_m = sb("deg_m", [P, G])
        w0 = [sb(f"w0_{h}", [P, C, 2 * D], F16) for h in ("hi", "lo")]
        w1 = [sb(f"w1_{h}", [P, C, 3 * D + 2], F16) for h in ("hi", "lo")]
        ident_s = sb("ident_s", [P, P], F16)
        bias1 = sb("bias1", [P, D], F16)
        ones1 = sb("ones1", [P, P], F16)
        w2 = [sb(f"w2_{h}", [P, C, 2 * D], F16) for h in ("hi", "lo")]
        w3 = [sb(f"w3_{h}", [P, C, 3 * P], F16) for h in ("hi", "lo")]
        mask_t = sb("mask_t", [P, G])
        logit_c = sb("logit_c", [P, G])
        logit_d = sb("logit_d", [P, G])
        score_c = sb("score_c", [P, 1])
        ident = sb("ident", [P, P])
        ident16 = sb("ident16", [P, P], F16)
        minus_half = sb("minus_half", [P, QUAD])

        stages = [t[:].rearrange("p g h n -> p (g h n)") for t in (am_t, an_t)]
        at_word = [0, P * G // 2]

        def staged(words, where=0):
            a = 2 * at_word[where]
            at_word[where] += words
            assert at_word[where] <= G * P
            return stages[where][:, a:a + 2 * words].bitcast(F32)

        w0_nat = staged(C * 2 * D).rearrange("p (c f) -> p c f", c=C)
        mask_nat = staged(P)
        assert at_word[0] <= 2 * U * P
        at_word[0] = 2 * U * P
        wk_f = staged(C * 3 * D).rearrange("p (c k f) -> p c k f", c=C, k=3)
        wv1_f = staged(C * D).rearrange("p (c f) -> p c f", c=C)
        wqk2_nat = staged(C * 2 * D).rearrange("p (c f) -> p c f", c=C)
        wqk2_t = staged(4 * D).rearrange("p (a d) -> p a d", a=4)
        w2_f = staged(C * 2 * D).rearrange("p (c f) -> p c f", c=C)
        wqk3_nat = staged(D)
        w3_f = staged(C * 3 * P).rearrange("p (c f) -> p c f", c=C)
        bcast = staged(4 * D, 1)
        wv3_nat = staged(C * D, 1).rearrange("p (c f) -> p c f", c=C)
        prod = staged(6 * D, 1).rearrange("p (k f) -> p k f", k=6)
        shared = sb("shared", [P, 2 * (P * 4 + (D + P) * 4 + D * 4)], F16)
        taken = [0, 0, 0]

        def ring_of(layer, shape, dt=F32):
            size = 2 // (1 if dt == F32 else 2)
            for n in shape:
                size *= n
            at = taken[layer]
            taken[layer] += size
            flat = shared[:, at:at + size]
            flat = flat.bitcast(F32) if dt == F32 else flat
            names = "abc"[:len(shape)]
            sizes = dict(zip(names[1:], shape[1:]))
            return flat.rearrange(f"p ({' '.join(names)}) -> p {' '.join(names)}", **sizes)

        an = ring_of(0, [2, P])
        am_f = ring_of(0, [2, P])
        xt0 = ring_of(0, [2, 2, D], F16)
        at_f = ring_of(0, [4, P])
        hr0 = ring_of(0, [2, D])
        y0 = ring_of(0, [2, D])
        vcols = sb("vcols", [P, C, 2])
        bsum = sb("bsum", [P, 4])

        parts = sb("parts", [P, 2, 4, D], F16)
        hi, lo = parts[:, 0], parts[:, 1]
        x_fixed = parts[:].rearrange("p h r d -> p (h r d)").bitcast(F32).rearrange("p (r d) -> p r d", r=4)
        xt = sb("xt", [P, 8, 4, P], F16)
        xt_f = xt[:].rearrange("p r c n -> p (r c n)").bitcast(F32)
        rows = xt_f[0:1, 0:4 * D + 2]
        bk_rows = xt_f[0:1, 4 * D + 2:7 * D + 2]
        ones_row = sb("ones_row", [1, P])
        dg = sb("dg", [P, 2, QUAD])
        rdeg = sb("rdeg", [P, 2, QUAD])
        sj = sb("sj", [P, 2, 2], F16)
        u = ring_of(1, [2, P])
        lk = ring_of(1, [2, P])
        ex = ring_of(1, [2, P])
        alpha = ring_of(1, [2, P])
        asum = sb("asum", [P, 2, 1])
        rsum = sb("rsum", [P, 2, 1])
        rinv = sb("rinv", [P, 2, 1])
        tr = ring_of(1, [2, 2, P], F16)
        tr_t = ring_of(1, [2, 2, P], F16)
        zh = ring_of(1, [2, 2, D], F16)
        yh = ring_of(1, [2, 2, D], F16)
        hr = ring_of(1, [2, D])
        kh = ring_of(2, [2, 2, ATT], F16)
        qs = ring_of(2, [2, ATT])
        dots = sb("dots", [P, 2, QUAD])
        logits = sb("logits", [P, 2, QUAD])
        pmax = sb("pmax", [QUAD, 2, 1])
        nmax = sb("nmax", [QUAD, 2, 1])
        pexp = ring_of(2, [2, P])[0:QUAD]
        psums = sb("psums", [QUAD, 2, 1])
        pinv = sb("pinv", [QUAD, 2, 1])
        prow = ring_of(2, [2, P])[0:QUAD]
        pcol = sb("pcol", [P, 2, QUAD])
        junk = ring_of(2, [2, D])
        assert taken[2] <= taken[1] - 2 * 2 * D

        bst = sb("bst", [P, 8, 6])
        mv = sb("mv", [P, 2, QUAD, 2])
        veps = sb("veps", [P, 2, QUAD])
        rstd = sb("rstd", [P, 2, QUAD])
        nb = sb("nb", [P, 2, QUAD])

        bank = [ctx.enter_context(nc.psum_tensor(f"bank{i}", [P, 512], F32)) for i in range(8)]
        bank16 = [b[:].bitcast(F16) for b in bank]

        x_loaded = [sem(f"x_loaded{i}") for i in range(QUEUE)]
        a_loaded = [sem(f"a_loaded{i}") for i in range(QUEUE)]
        w0_loaded = sem("w0_loaded")
        w_loaded = sem("w_loaded")
        stored = sem("stored")
        ident_ready = sem("ident_ready")
        pool_ready = sem("pool_ready")
        w0_turned = sem("w0_turned")
        w0_ready = sem("w0_ready")
        prep_pe = sem("prep_pe")
        prep_dve = sem("prep_dve")
        prep_act = sem("prep_act")

        deg_done = sem("deg_done")
        degm_done = sem("degm_done")
        rdeg_done = sem("rdeg_done")
        x_fixed_done = sem("x_fixed_done")
        an_done = sem("an_done")
        tr0_done = sem("tr0_done")
        amf_done = sem("amf_done")
        at_done = sem("at_done")
        xlo_done = sem("xlo_done")
        relu0_done = sem("relu0_done")
        ahi_done = sem("ahi_done")
        alo_done = sem("alo_done")
        xw0_done = sem("xw0_done")
        y0_done = sem("y0_done")
        ay_done = sem("ay_done")

        coef_done = sem("coef_done")
        hi_done = [None] + [sem(f"hi_done{n}") for n in (1, 2, 3)]
        lo_done = [None] + [sem(f"lo_done{n}") for n in (1, 2, 3)]
        trx_done = [None] + [sem(f"trx_done{n}") for n in (1, 2, 3)]
        xt_done = [None] + [sem(f"xt_done{n}") for n in (1, 2, 3)]

        xwb_done = sem("xwb_done")
        xwa_done = sem("xwa_done")
        sjhi_done = sem("sjhi_done")
        sjlo_done = sem("sjlo_done")
        sj_spread = sem("sj_spread")
        u_done = sem("u_done")
        lk_done = sem("lk_done")
        ex_done = sem("ex_done")
        alpha_done = sem("alpha_done")
        rsum_done = sem("rsum_done")
        rinv_done = sem("rinv_done")
        thi_done = sem("thi_done")
        tlo_done = sem("tlo_done")
        trt_done = sem("trt_done")
        tt_done = sem("tt_done")
        yhi_done = sem("yhi_done")
        ylo_done = sem("ylo_done")
        ty_done = sem("ty_done")
        zhi_done = sem("zhi_done")
        zlo_done = sem("zlo_done")
        tz_done = sem("tz_done")
        relu_done = sem("relu_done")

        qx_done = [None, None, sem("xm_done"), sem("qk_done")]
        ax_done = [None, None, sem("ax_done"), sem("ak_done")]
        q_saved = [None, None, sem("xm_saved"), sem("q_saved")]
        khi_done = sem("khi_done")
        klo_done = sem("klo_done")
        dot_done = [None, None, sem("dot_done2"), sem("dot_done3")]
        logit_done = [None, None, sem("logit_done2"), sem("logit_done3")]
        turned = [None, None, sem("turned2"), sem("turned3")]
        pmax_done = [None, None, sem("pmax_done2"), sem("pmax_done3")]
        nmax_done = [None, None, sem("nmax_done2"), sem("nmax_done3")]
        pexp_done = [None, None, sem("pexp_done2"), sem("pexp_done3")]
        pinv_done = [None, None, sem("pinv_done2"), sem("pinv_done3")]
        prow_done = [None, None, sem("prow_done2"), sem("prow_done3")]
        pback = [None, None, sem("pback2"), sem("pback3")]
        pcol_done = [None, None, sem("pcol_done2"), sem("pcol_done3")]
        v_done = [None, None, sem("v_done2"), sem("v_done3")]

        res_done = [sem(f"res_done{n}") for n in range(4)]
        stats_done = [sem(f"stats_done{n}") for n in range(4)]
        aggr_done = [sem(f"aggr_done{n}") for n in range(4)]
        veps_done = [sem(f"veps_done{n}") for n in range(4)]
        rstd_done = [sem(f"rstd_done{n}") for n in range(4)]
        nb_done = [sem(f"nb_done{n}") for n in range(4)]
        norm_done = [sem(f"norm_done{n}") for n in range(4)]
        norm_even = sem("norm_even")

        hi_last = [None, trx_done[1], ax_done[2], trx_done[3]]
        xt_last = [None, xwa_done, v_done[2], v_done[3]]
        RES_LAG = [1, 1, 7, 7]
        NORM_LAG = [r + 7 for r in RES_LAG]

        block = ctx.enter_context(nc.Block())

        @block.sync
        def _(sp):
            def load(q, i):
                sp.dma_start(adj[:, bass.ds(q * QUAD, QUAD), :],
                             adj_in[bass.ds(q * QUAD, QUAD)].rearrange("g n m -> n g m"))\
                    .then_inc(a_loaded[i], 16)
                sp.dma_start(x[:, bass.ds(q * QUAD, QUAD), :],
                             x_in[bass.ds(q * QUAD, QUAD)].rearrange("g n d -> n g d"))\
                    .then_inc(x_loaded[i], 16)

            for i in range(QUEUE):
                load(i, i)
            loads = [
                (rows[:, 0:2 * D], aw1_in.rearrange("(a n) -> a n", a=1)),
                (rows[:, 2 * D:3 * D], bv1_in.rearrange("(a n) -> a n", a=1)),
                (rows[:, 4 * D:4 * D + 1], ab1_in.rearrange("(a n) -> a n", a=1)),
                (bk_rows, bk1_in.rearrange("(a k) n -> a (k n)", a=1)),
                (wv1_f, wv1_in.rearrange("(c p) f -> p c f", p=P)),
                (wqk2_nat, wqk2_in.rearrange("(c p) f -> p c f", p=P)),
                (w2_f[:, :, D:2 * D], wv2_in.rearrange("(c p) f -> p c f", p=P)),
                (wqk3_nat, wqk3_in),
                (wv3_nat, wv3_in.rearrange("(c p) f -> p c f", p=P)),
            ] + [(wk_f[:, :, k, :], wk1_in[k].rearrange("(c p) f -> p c f", p=P)) for k in range(3)]
            for dst, src in loads:
                sp.dma_start(dst, src).then_inc(w_loaded, 16)
            assert len(loads) == N_LOADS
            with sp.Fori(1, G // QUAD // QUEUE) as r:
                for i in range(QUEUE):
                    sp.wait_ge(a_loaded[i], 16 * r)
                    sp.wait_ge(x_loaded[i], 16 * r)
                    load(r * QUEUE + i, i)
            with sp.Fori(0, G // 2) as h:
                sp.wait_ge(norm_done[3], 2 * h + 2)
                sp.wait_ge(norm_even, 2 * h + 2)
                sp.dma_start(out[bass.ds(h * 2, 2)].rearrange("g n d -> n g d"),
                             x[:, bass.ds(h * 2, 2), :]).then_inc(stored, 16)
            sp.wait_ge(stored, 16 * (G // 2))

        @block.gpsimd
        def _(pool):
            nc.gpsimd.memset(ident[:], 0.0).then_inc(ident_ready, 1)
            nc.gpsimd.memset(ident16[:], 0.0).then_inc(ident_ready, 1)
            pool.wait_ge(ident_ready, 2)
            for m in (ident, ident16):
                nc.gpsimd.affine_select(out=m[:], in_=m[:], compare_op=ALU.not_equal, fill=1.0, base=0,
                                        pattern=[[-1, P]], channel_multiplier=1).then_inc(ident_ready, 1)
            nc.gpsimd.memset(minus_half[:], -0.5).then_inc(pool_ready, 1)
            pool.wait_ge(pool_ready, 1)
            nc.gpsimd.tensor_tensor(rstd[:, 0, :], minus_half[:], minus_half[:], ALU.mult).then_inc(pool_ready, 1)
            pool.wait_ge(pool_ready, 2)

            def inverse_root(n, g):
                if g is None or g.pos % QUAD != QUAD - 1:
                    return
                r = g.ring(8) // QUAD
                wait(pool, veps_done[n], g.count())
                wait_back(pool, norm_done[n], g, 8, norm_done[n - 1] if n else None)
                if n == 3:
                    wait_back(pool, norm_even, g, 8)
                nc.gpsimd.tensor_tensor(rstd[:, r, :], veps[:, r, :], minus_half[:], ALU.pow)\
                    .then_inc(rstd_done[n], QUAD)

            def step0(s):
                if g := s.item(2):
                    wait(pool, ahi_done, g.count())
                    nc.gpsimd.tensor_tensor(an_t[:, g.index, 1, :], at_f[:, g.ring(4), :],
                                            an_t[:, g.index, 0, :], ALU.subtract)
                    nc.gpsimd.tensor_tensor(am_t[:, g.index, 1, :], am_f[:, g.ring(2), :],
                                            am_t[:, g.index, 0, :], ALU.subtract).then_inc(alo_done, 1)
                inverse_root(0, s.item(-RES_LAG[0] - 1))

            def later_step(n, lead):
                def step(s):
                    if n == 1 and (g := s.item(-1)):
                        pool.wait_ge(pool_ready, 2)
                        wait(pool, relu_done, g.count())
                        nc.gpsimd.tensor_tensor(x[:, g.index, :], x[:, g.index, :], hr[:, g.ring(2), :],
                                                ALU.add).then_inc(res_done[1], 1)
                    if g := s.item(lead):
                        if n == 1 and isinstance(g.index, int) and g.index < 4:
                            pool.wait_ge(tr0_done, G - 1 + g.index // 2)
                        wait(pool, hi_done[n], g.count())
                        nc.gpsimd.tensor_tensor(lo[:, g.ring(4), :], x[:, g.index, :], hi[:, g.ring(4), :],
                                                ALU.subtract).then_inc(lo_done[n], 1)
                    inverse_root(n, s.item(-RES_LAG[n] - 1))
                return step

            run_layers(pool, [(2, RES_LAG[0] + 1, step0, 2), (4, RES_LAG[1] + 1, later_step(1, 4), 2),
                              (3, RES_LAG[2] + 1, later_step(2, 3), 2), (3, RES_LAG[3] + 1, later_step(3, 3), 2)])

        @block.scalar
        def _(act):
            act.dma_start(w0_nat, w0_in.rearrange("(c p) f -> p c f", p=P)).then_inc(w0_loaded, 16)
            act.dma_start(mask_nat[0:G, :], mask_in).then_inc(w0_loaded, 16)
            nc.scalar.preload_act_table(ACT.Exp)

            for c in range(C):
                act.wait_ge(w0_turned, c + 1)
                nc.scalar.activation(w0[0][:, c, :], bank[6 + c][:], ACT.Copy, scale=SCALE).then_inc(prep_act, 1)
            act.wait_ge(prep_pe, 1)
            nc.scalar.activation(mask_t[:], bank[5][:, 0:G], ACT.Copy).then_inc(prep_act, 1)
            act.wait_ge(prep_act, 3)

            def prepare(s):
                if s.at(3):
                    act.wait_ge(w_loaded, 16 * N_LOADS)
                    nc.scalar.activation(w1[0][:, :, 0:3 * D], wk_f.rearrange("p c k f -> p c (k f)"),
                                         ACT.Copy, scale=SCALE).then_inc(prep_act, 1)
                if s.at(4):
                    act.wait_ge(prep_pe, 2)
                    nc.scalar.activation(bcast[:, 0:2 * D], bank[6][:], ACT.Copy).then_inc(prep_act, 1)
                if s.at(5):
                    act.wait_ge(prep_pe, 3)
                    nc.scalar.activation(bcast[:, 2 * D:4 * D], bank[7][:], ACT.Copy).then_inc(prep_act, 1)
                if s.at(6):
                    act.wait_ge(prep_pe, 4)
                    nc.scalar.activation(bsum[:, 3:4], bank[6][:, 0:1], ACT.Copy).then_inc(prep_act, 1)
                if s.at(7):
                    act.wait_ge(prep_pe, 5)
                    nc.scalar.activation(wqk2_t[:, 0:2, :].rearrange("p a d -> p (a d)"), bank[7][:],
                                         ACT.Copy).then_inc(prep_act, 1)
                if s.at(8):
                    act.wait_ge(prep_pe, 6)
                    nc.scalar.activation(wqk2_t[:, 2:4, :].rearrange("p a d -> p (a d)"), bank[6][:],
                                         ACT.Copy).then_inc(prep_act, 1)
                if s.at(9):
                    act.wait_ge(prep_pe, 7)
                    nc.scalar.activation(w3_f[:, :, P:3 * P], bank[7][:].rearrange("p (c e) -> p c e", c=C),
                                         ACT.Copy).then_inc(prep_act, 1)
                if s.at(10):
                    act.wait_ge(prep_pe, 8)
                    nc.scalar.activation(w3_f[:, :, 0:P], bank[6][:, 0:C * P].rearrange("p (c e) -> p c e", c=C),
                                         ACT.Copy).then_inc(prep_act, 1)
                    act.wait_ge(prep_act, 11)
                    nc.scalar.activation(w3[0][:], w3_f, ACT.Copy, scale=SCALE).then_inc(prep_act, 1)
                if s.at(11):
                    act.wait_ge(prep_pe, 9)
                    nc.scalar.activation(w2_f[:, :, 0:D], bank[7][:].rearrange("p (c e) -> p c e", c=C),
                                         ACT.Copy).then_inc(prep_act, 1)
                    act.wait_ge(prep_act, 13)
                    nc.scalar.activation(w2[0][:], w2_f, ACT.Copy, scale=SCALE).then_inc(prep_act, 1)
                if s.at(14):
                    act.wait_ge(prep_act, PREP_ACT)
                    act.wait_ge(prep_dve, PREP_DVE)

            def step0(s):
                prepare(s)
                if g := s.item(0):
                    wait(act, xw0_done, g.count())
                    nc.scalar.activation(y0[:, g.ring(2), :], bank[2 + g.ring(4)][:, D:2 * D], ACT.Copy,
                                         scale=1.0 / SCALE).then_inc(y0_done, 1)
                if g := s.item(-1):
                    wait(act, ay_done, g.count())
                    wait(act, res_done[0], g.count(2))
                    nc.scalar.activation(hr0[:, g.ring(2), :], bank[2 + g.ring(4)][:, 0:D], ACT.Relu,
                                         scale=1.0 / (X_SCALE * SCALE)).then_inc(relu0_done, 1)
                if g := s.item(2):
                    b = bank[g.ring(2)]
                    wait(act, tr0_done, g.count())
                    nc.scalar.activation(xt0[:, g.ring(2), 0, :], b[:, 0:D], ACT.Copy, scale=X_SCALE)
                    wait(act, alo_done, g.count(2))
                    nc.scalar.activation(at_f[:, g.ring(4), :], b[:, D:D + P], ACT.Copy).then_inc(at_done, 1)
                    nc.scalar.activation(am_f[:, g.ring(2), :], b[:, D:D + P], ACT.Copy,
                                         scale=mask_t[:, bass.ds(g.index, 1)]).then_inc(amf_done, 1)
                    wait(act, at_done, g.count())
                    nc.scalar.activation(an_t[:, g.index, 0, :], at_f[:, g.ring(4), :], ACT.Copy)
                    wait(act, amf_done, g.count())
                    nc.scalar.activation(am_t[:, g.index, 0, :], am_f[:, g.ring(2), :], ACT.Copy)\
                        .then_inc(ahi_done, 1)
                if g := s.item(4):
                    if g.pos % QUAD == 0:
                        act.wait_ge(x_loaded[g.pos // QUAD], (g.index - g.pos) * 2 + 16)
                    wait(act, tr0_done, g.count(4))
                    nc.scalar.activation(x_fixed[:, g.ring(4), :], x[:, g.index, :], ACT.Copy)\
                        .then_inc(x_fixed_done, 1)

            def split_hi(n, g):
                wait(act, norm_done[n - 1], g.count())
                if n == 1 and isinstance(g.index, int) and g.index < 4:
                    act.wait_ge(tr0_done, G - 3 + g.index // 2)
                wait_back(act, hi_last[n], g, 4, hi_last[n - 1])
                nc.scalar.activation(hi[:, g.ring(4), :], x[:, g.index, :], ACT.Copy).then_inc(hi_done[n], 1)

            def save_xt(n, g, last_reader, depth=8):
                wait(act, trx_done[n], g.count())
                wait_back(act, last_reader[n], g, depth, last_reader[n - 1])
                nc.scalar.activation(xt[:, g.ring(8), :, :].rearrange("p c n -> p (c n)"),
                                     bank16[g.ring(2)][:, 0:4 * P], ACT.Copy).then_inc(xt_done[n], 1)

            def step1(s):
                if g := s.item(0):
                    wait(act, trt_done, g.count())
                    wait(act, tz_done, g.count(2))
                    nc.scalar.activation(tr_t[:, g.ring(2), :, :].rearrange("p h n -> p (h n)"),
                                         bank16[6 + g.ring(2)][:, 0:2 * P], ACT.Copy).then_inc(tt_done, 1)
                if g := s.item(-1):
                    wait(act, tz_done, g.count())
                    wait(act, res_done[1], g.count(2))
                    nc.scalar.activation(hr[:, g.ring(2), :], bank[4 + g.ring(2)][:, 0:D], ACT.Relu,
                                         scale=1.0 / SCALE).then_inc(relu_done, 1)
                if g := s.item(3):
                    save_xt(1, g, xt_last)
                if g := s.item(2):
                    wait(act, xwb_done, g.count())
                    nc.scalar.activation(sj[:, g.ring(2), 0:1], bank[2 + g.ring(2)][:, D + 1:D + 2], ACT.Copy,
                                         scale=1.0 / SCALE).then_inc(sjhi_done, 1)
                if g := s.item(4):
                    split_hi(1, g)
                if g := s.item(0):
                    wait(act, ty_done, g.count())
                    nc.scalar.activation(zh[:, g.ring(2), 0, :], bank[4 + g.ring(2)][:, D:2 * D], ACT.Copy,
                                         scale=1.0 / SCALE).then_inc(zhi_done, 1)
                if g := s.item(2):
                    wait(act, u_done, g.count())
                    wait(act, ty_done, g.count(2))
                    nc.scalar.activation(yh[:, g.ring(2), 0, :], bank[2 + g.ring(2)][:, 0:D], ACT.Copy,
                                         scale=1.0 / SCALE).then_inc(yhi_done, 1)
                    wait(act, lk_done, g.count())
                    wait(act, alpha_done, g.count(2))
                    nc.scalar.activation(ex[:, g.ring(2), :], lk[:, g.ring(2), :], ACT.Exp,
                                         scale=1.0 / PROD).then_inc(ex_done, 1)

            def softmax_exp(n, g):
                r = g.ring(8) // QUAD
                wait(act, nmax_done[n], g.count())
                wait_back(act, pback[n], g, 8, pback[n - 1])
                nc.scalar.activation(pexp[:, r, :], bank[7][0:QUAD, 0:P], ACT.Exp, bias=nmax[:, r, :],
                                     accum_out=psums[:, r, :]).then_inc(pexp_done[n], QUAD)

            def step2(s):
                if g := s.item(3):
                    split_hi(2, g)
                if g := s.item(1):
                    wait(act, qx_done[2], g.count())
                    wait_back(act, dot_done[2], g, 2, res_done[1])
                    nc.scalar.activation(hr[:, g.ring(2), :], bank[2 + g.ring(2)][:, 0:D], ACT.Copy)\
                        .then_inc(q_saved[2], 1)
                if (g := s.item(-2)) and g.pos % QUAD == QUAD - 1:
                    softmax_exp(2, g)
                if g := s.item(2):
                    save_xt(2, g, xt_last)

            def step3(s):
                if g := s.item(3):
                    split_hi(3, g)
                if (g := s.item(-NORM_LAG[3])) and g.pos % 2 == 0:
                    r, k = g.ring(8) // QUAD, g.ring(QUAD)
                    wait(act, nb_done[3], g.count(-(QUAD - 1 - k)))
                    nc.scalar.activation(x[:, g.index, :], x[:, g.index, :], ACT.Identity,
                                         bias=nb[:, r, k:k + 1], scale=rstd[:, r, k:k + 1])\
                        .then_inc(norm_even, 2)
                if g := s.item(1):
                    wait(act, qx_done[3], g.count())
                    wait(act, dot_done[3], g.count(2))
                    nc.scalar.activation(qs[:, g.ring(2), :], bank[2 + g.ring(2)][:, 0:ATT], ACT.Copy)\
                        .then_inc(q_saved[3], 1)
                    nc.scalar.activation(kh[:, g.ring(2), 0, :], bank[2 + g.ring(2)][:, ATT:2 * ATT], ACT.Copy,
                                         scale=1.0 / SCALE).then_inc(khi_done, 1)
                if (g := s.item(-2)) and g.pos % QUAD == QUAD - 1:
                    softmax_exp(3, g)
                if g := s.item(2):
                    save_xt(3, g, xt_last)

            run_layers(act, [(4, 1, step0, 2), (4, 1, step1, 1), (3, 2, step2, 2), (3, NORM_LAG[3], step3, 2)])

        @block.vector
        def _(dve):
            v = nc.vector
            v.memset(ones1[:], 1.0).then_inc(prep_dve, 1)
            v.memset(ones_row[:], 1.0).then_inc(prep_dve, 1)
            v.memset(rows[:, 4 * D + 1:4 * D + 2], 0.0).then_inc(prep_dve, 1)

            def prepare(s):
                if s.at(-2):
                    for c in range(C):
                        dve.wait_ge(prep_act, c + 1)
                        v.scalar_tensor_tensor(out=w0[1][:, c, :], in0=bank[6 + c][:], scalar=SCALE,
                                               in1=w0[0][:, c, :], op0=ALU.mult, op1=ALU.subtract)\
                            .then_inc(w0_ready, 1)
                if s.at(3):
                    dve.wait_ge(w_loaded, 16 * N_LOADS)
                    v.tensor_tensor(bk_rows[:, 0:D], bk_rows[:, 0:D], bk_rows[:, D:2 * D], ALU.add)\
                        .then_inc(prep_dve, 1)
                    dve.wait_ge(prep_dve, 4)
                    v.tensor_tensor(rows[:, 3 * D:4 * D], bk_rows[:, 0:D], bk_rows[:, 2 * D:3 * D], ALU.add)\
                        .then_inc(prep_dve, 1)
                for c in range(C):
                    if s.at(5 + c):
                        dve.wait_ge(prep_act, 4)
                        v.scalar_tensor_tensor(out=w1[1][:, c, 0:3 * D],
                                               in0=wk_f[:, c].rearrange("p k f -> p (k f)"), scalar=SCALE,
                                               in1=w1[0][:, c, 0:3 * D], op0=ALU.mult, op1=ALU.subtract)\
                            .then_inc(prep_dve, 1)
                for j in range(2):
                    if s.at(7 + j):
                        dve.wait_ge(prep_act, 7)
                        for c in range(C):
                            v.scalar_tensor_tensor(out=prod[:, 3 * j + c, :], in0=wv1_f[:, c, :], scalar=SCALE,
                                                   in1=bcast[:, j * D:(j + 1) * D], op0=ALU.mult, op1=ALU.mult,
                                                   accum_out=vcols[:, c, 1 - j:2 - j]).then_inc(prep_dve, 1)
                        v.scalar_tensor_tensor(out=prod[:, 3 * j + 2, :], in0=bcast[:, 2 * D:3 * D], scalar=1.0,
                                               in1=bcast[:, j * D:(j + 1) * D], op0=ALU.mult, op1=ALU.mult,
                                               accum_out=bsum[:, j:j + 1]).then_inc(prep_dve, 1)
                if s.at(9):
                    dve.wait_ge(prep_dve, 13)
                    v.tensor_tensor(bsum[:, 2:3], bsum[:, 0:1], bsum[:, 1:2], ALU.add).then_inc(prep_dve, 1)
                    v.tensor_copy(w1[0][:, :, 3 * D:3 * D + 2], vcols[:]).then_inc(prep_dve, 1)
                    dve.wait_ge(prep_dve, 15)
                    v.tensor_scalar(score_c[:], bsum[:, 2:3], bsum[:, 3:4], PROD, ALU.add, ALU.mult)\
                        .then_inc(prep_dve, 1)
                    v.tensor_tensor(w1[1][:, :, 3 * D:3 * D + 2], vcols[:], w1[0][:, :, 3 * D:3 * D + 2],
                                    ALU.subtract).then_inc(prep_dve, 1)
                if s.at(10):
                    dve.wait_ge(ident_ready, 4)
                    v.tensor_scalar(ident_s[:], ident16[:], SCALE, None, ALU.mult).then_inc(prep_dve, 1)
                if s.at(11):
                    v.tensor_scalar(bias1[:], bcast[:, 3 * D:4 * D], SCALE, None, ALU.mult)\
                        .then_inc(prep_dve, 1)
                    dve.wait_ge(prep_dve, 19)
                    v.tensor_copy(prod[P // 2:P, 0, :], bias1[P // 2:P, :]).then_inc(prep_dve, 1)
                    dve.wait_ge(prep_dve, 20)
                    v.scalar_tensor_tensor(out=bias1[P // 2:P, :], in0=bcast[P // 2:P, 3 * D:4 * D],
                                           scalar=SCALE, in1=prod[P // 2:P, 0, :], op0=ALU.mult,
                                           op1=ALU.subtract).then_inc(prep_dve, 1)
                if s.at(12):
                    dve.wait_ge(prep_act, 12)
                    v.scalar_tensor_tensor(out=w3[1][:], in0=w3_f, scalar=SCALE, in1=w3[0][:],
                                           op0=ALU.mult, op1=ALU.subtract).then_inc(prep_dve, 1)
                if s.at(13):
                    dve.wait_ge(prep_act, PREP_ACT)
                    v.scalar_tensor_tensor(out=w2[1][:], in0=w2_f, scalar=SCALE, in1=w2[0][:],
                                           op0=ALU.mult, op1=ALU.subtract).then_inc(prep_dve, 1)
                    dve.wait_ge(prep_dve, PREP_DVE)

            def norm_stats(n, s):
                if g := s.item(-RES_LAG[n]):
                    dve.wait_ge(prep_dve, 1)
                    wait(dve, res_done[n], g.count())
                    v.bn_stats(bst[:, g.ring(8), :], x[:, g.index, :]).then_inc(stats_done[n], 1)

            def norm_aggr(n, s):
                if g := s.item(-RES_LAG[n] - 1):
                    dve.wait_ge(prep_dve, 1)
                    wait(dve, stats_done[n], g.count())
                    v.bn_aggr(mv[:, g.ring(8) // QUAD, g.ring(QUAD), :], bst[:, g.ring(8), :])\
                        .then_inc(aggr_done[n], 1)

            def norm_veps(n, s):
                scale2 = 1.0 if n == 0 else PROD
                to = 1.0 / PROD if n < 3 else 1.0
                if (g := s.item(-RES_LAG[n] - 1)) and g.pos % QUAD == QUAD - 1:
                    r = g.ring(8) // QUAD
                    wait(dve, aggr_done[n], g.count())
                    v.tensor_scalar(veps[:, r, :], mv[:, r, :, 1], scale2 * LN_EPS, to, ALU.add, ALU.mult)\
                        .then_inc(veps_done[n], QUAD)

            def norm_apply(n, s):
                if (g := s.item(-NORM_LAG[n])) and (n < 3 or g.pos % 2):
                    r, k = g.ring(8) // QUAD, g.ring(QUAD)
                    wait(dve, nb_done[n], g.count(-(QUAD - 1 - k)))
                    v.tensor_scalar(x[:, g.index, :], x[:, g.index, :], rstd[:, r, k:k + 1],
                                    nb[:, r, k:k + 1], ALU.mult, ALU.add).then_inc(norm_done[n], 2 if n == 3 else 1)
                if (g := s.item(-RES_LAG[n] - 3)) and g.pos % QUAD == QUAD - 1:
                    r = g.ring(8) // QUAD
                    wait(dve, rstd_done[n], g.count())
                    v.scalar_tensor_tensor(out=nb[:, r, :], in0=mv[:, r, :, 0], scalar=-1.0,
                                           in1=rstd[:, r, :], op0=ALU.mult, op1=ALU.mult)\
                        .then_inc(nb_done[n], QUAD)

            def step0(s):
                prepare(s)
                if g := s.item(3):
                    r, k = g.pos // QUAD, g.pos % QUAD
                    wait(dve, rdeg_done, g.count(k + 1 - QUAD))
                    wait(dve, tr0_done, g.count(2))
                    v.tensor_scalar(an[:, g.ring(2), :], adj[:, g.index, :], rdeg[:, r, k:k + 1], SCALE,
                                    ALU.mult, ALU.mult).then_inc(an_done, 1)
                quad = (g := s.item(4)) and g.pos % QUAD == 0 and g
                if g := quad:
                    r = g.pos // QUAD
                    dve.wait_ge(a_loaded[r], (g.index - g.pos) * 2 + 16)
                    v.tensor_reduce(dg[:, r, :], adj[:, bass.ds(g.index, QUAD), :], AX_X, ALU.add)\
                        .then_inc(deg_done, QUAD)
                if g := s.item(-1):
                    wait(dve, relu0_done, g.count())
                    v.tensor_tensor(x[:, g.index, :], x[:, g.index, :], hr0[:, g.ring(2), :], ALU.add)\
                        .then_inc(res_done[0], 1)
                if g := quad:
                    wait(dve, deg_done, g.count(1 - QUAD))
                    v.tensor_scalar(deg_m[:, bass.ds(g.index, QUAD)], dg[:, g.pos // QUAD, :], DEG_EPS, None,
                                    ALU.max).then_inc(degm_done, QUAD)
                norm_aggr(0, s)
                norm_apply(0, s)
                if g := quad:
                    wait(dve, degm_done, g.count(1 - QUAD))
                    v.reciprocal(rdeg[:, g.pos // QUAD, :], deg_m[:, bass.ds(g.index, QUAD)])\
                        .then_inc(rdeg_done, QUAD)
                norm_stats(0, s)
                norm_veps(0, s)
                if g := s.item(2):
                    wait(dve, amf_done, g.count())
                    v.scalar_tensor_tensor(out=xt0[:, g.ring(2), 1, :], in0=bank[g.ring(2)][:, 0:D],
                                           scalar=X_SCALE, in1=xt0[:, g.ring(2), 0, :],
                                           op0=ALU.mult, op1=ALU.subtract).then_inc(xlo_done, 1)

            def step1(s):
                if s.at(-2):
                    dve.wait_ge(alo_done, G)
                if s.pos == 0 and (g := s.item(-2)):
                    wait(dve, res_done[1], g.count())
                norm_apply(1, s)
                norm_aggr(1, s)
                if g := s.item(1):
                    r = g.ring(2)
                    wait(dve, ex_done, g.count())
                    v.scalar_tensor_tensor(out=alpha[:, r, :], in0=adj[:, g.index, :], scalar=1.0,
                                           in1=ex[:, r, :], op0=ALU.mult, op1=ALU.mult,
                                           accum_out=asum[:, r, :]).then_inc(alpha_done, 1)
                norm_veps(1, s)
                if g := s.item(1):
                    wait(dve, yhi_done, g.count())
                    v.scalar_tensor_tensor(out=yh[:, r, 1, :], in0=bank[2 + r][:, 0:D], scalar=1.0 / SCALE,
                                           in1=yh[:, r, 0, :], op0=ALU.mult, op1=ALU.subtract)\
                        .then_inc(ylo_done, 1)
                    wait(dve, alpha_done, g.count())
                    v.tensor_scalar(rsum[:, r, :], asum[:, r, :], ROW_EPS, 1.0 / SCALE, ALU.add, ALU.mult)\
                        .then_inc(rsum_done, 1)
                if g := s.item(1):
                    r = g.ring(2)
                    wait(dve, rsum_done, g.count())
                    v.reciprocal(rinv[:, r, :], rsum[:, r, :]).then_inc(rinv_done, 1)
                if g := s.item(2):
                    wait(dve, sjhi_done, g.count())
                    v.scalar_tensor_tensor(out=sj[:, g.ring(2), 1:2], in0=bank[2 + g.ring(2)][:, D + 1:D + 2],
                                           scalar=1.0 / SCALE, in1=sj[:, g.ring(2), 0:1],
                                           op0=ALU.mult, op1=ALU.subtract).then_inc(sjlo_done, 1)
                if g := s.item(1):
                    r = g.ring(2)
                    wait(dve, rinv_done, g.count())
                    v.tensor_scalar(tr[:, r, 0, :], alpha[:, r, :], rinv[:, r, :], None, ALU.mult)\
                        .then_inc(thi_done, 1)
                if g := s.item(1):
                    r = g.ring(2)
                    wait(dve, thi_done, g.count())
                    v.scalar_tensor_tensor(out=tr[:, r, 1, :], in0=alpha[:, r, :], scalar=rinv[:, r, :],
                                           in1=tr[:, r, 0, :], op0=ALU.mult, op1=ALU.subtract)\
                        .then_inc(tlo_done, 1)
                if g := s.item(0):
                    wait(dve, zhi_done, g.count())
                    v.scalar_tensor_tensor(out=zh[:, g.ring(2), 1, :], in0=bank[4 + g.ring(2)][:, D:2 * D],
                                           scalar=1.0 / SCALE, in1=zh[:, g.ring(2), 0, :],
                                           op0=ALU.mult, op1=ALU.subtract).then_inc(zlo_done, 1)
                if g := s.item(2):
                    xwb = bank[2 + g.ring(2)]
                    wait(dve, sj_spread, g.count())
                    v.tensor_scalar(u[:, g.ring(2), :], xwb[:, D + 2:D + 2 + P], xwb[:, D:D + 1],
                                    score_c[:, 0:1], ALU.add, ALU.add).then_inc(u_done, 1)
                if g := s.item(2):
                    wait(dve, u_done, g.count())
                    v.scalar_tensor_tensor(out=lk[:, g.ring(2), :], in0=u[:, g.ring(2), :], scalar=SLOPE,
                                           in1=u[:, g.ring(2), :], op0=ALU.mult, op1=ALU.max)\
                        .then_inc(lk_done, 1)
                norm_stats(1, s)
                if s.at(7):
                    v.tensor_scalar(logit_d[:], deg_m[:], 1.0 / (8 * PROD * PROD), None, ALU.mult)\
                        .then_inc(coef_done, 1)
                    v.scalar_tensor_tensor(out=logit_c[:], in0=deg_m[:], scalar=1.0 / (16 * PROD * PROD),
                                           in1=mask_t[:], op0=ALU.mult, op1=ALU.mult).then_inc(coef_done, 1)
                    dve.wait_ge(coef_done, 2)

            def gate_steps(n, width, s):
                quad2 = (g := s.item(-2)) and g.pos % QUAD == QUAD - 1 and g
                quad3 = (g := s.item(-3)) and g.pos % QUAD == QUAD - 1 and g
                quad4 = (g := s.item(-4)) and g.pos % QUAD == QUAD - 1 and g
                if n == 3 and (g := s.item(0)):
                    wait(dve, khi_done, g.count())
                    v.scalar_tensor_tensor(out=kh[:, g.ring(2), 1, :], in0=bank[2 + g.ring(2)][:, ATT:2 * ATT],
                                           scalar=1.0 / SCALE, in1=kh[:, g.ring(2), 0, :],
                                           op0=ALU.mult, op1=ALU.subtract).then_inc(klo_done, 1)
                if g := quad2:
                    wait(dve, turned[n], g.count())
                    v.tensor_reduce(pmax[:, g.ring(8) // QUAD, :], bank[7][0:QUAD, 0:P], AX_X, ALU.max)\
                        .then_inc(pmax_done[n], QUAD)
                if g := quad4:
                    wait(dve, pback[n], g.count())
                    v.tensor_copy(pcol[:, g.ring(8) // QUAD, :], bank[7][:, P:P + QUAD])\
                        .then_inc(pcol_done[n], QUAD)
                norm_apply(n, s)
                if g := quad2:
                    r = g.ring(8) // QUAD
                    wait(dve, pmax_done[n], g.count())
                    v.tensor_scalar(nmax[:, r, :], pmax[:, r, :], -1.0, None, ALU.mult)\
                        .then_inc(nmax_done[n], QUAD)
                if g := quad3:
                    r = g.ring(8) // QUAD
                    wait(dve, pexp_done[n], g.count())
                    v.reciprocal(pinv[:, r, :], psums[:, r, :]).then_inc(pinv_done[n], QUAD)
                if g := s.item(-RES_LAG[n]):
                    r, k = g.ring(8) // QUAD, g.ring(QUAD)
                    wait(dve, v_done[n], g.count())
                    wait(dve, pcol_done[n], g.count(k + 1 - QUAD))
                    v.scalar_tensor_tensor(out=x[:, g.index, :], in0=bank[4 + g.ring(2)][:, 0:D],
                                           scalar=pcol[:, r, k:k + 1], in1=x[:, g.index, :],
                                           op0=ALU.mult, op1=ALU.add).then_inc(res_done[n], 1)
                if g := quad3:
                    r = g.ring(8) // QUAD
                    wait(dve, pinv_done[n], g.count())
                    v.tensor_scalar(prow[:, r, :], pexp[:, r, :], pinv[:, r, :], 1.0 / SCALE,
                                    ALU.mult, ALU.mult).then_inc(prow_done[n], QUAD)
                if s.pos == 0 and (g := s.item(-RES_LAG[n] - 1)):
                    wait(dve, res_done[n], g.count())
                if g := s.item(0):
                    r, k = g.ring(8) // QUAD, g.ring(QUAD)
                    wait(dve, ax_done[n], g.count())
                    wait(dve, q_saved[n], g.count())
                    v.scalar_tensor_tensor(out=junk[:, g.ring(2), 0:width],
                                           in0=bank[2 + g.ring(2)][:, D:D + width], scalar=1.0,
                                           in1=(hr if n == 2 else qs)[:, g.ring(2), :],
                                           op0=ALU.mult, op1=ALU.mult, accum_out=dots[:, r, k:k + 1])\
                        .then_inc(dot_done[n], 1)
                norm_aggr(n, s)
                norm_stats(n, s)
                norm_veps(n, s)
                if (g := s.item(0)) and g.pos % QUAD == QUAD - 1:
                    r = g.ring(8) // QUAD
                    wait(dve, dot_done[n], g.count())
                    v.tensor_tensor(logits[:, r, :], dots[:, r, :],
                                    (logit_c if n == 2 else logit_d)[:, bass.ds(g.index - (QUAD - 1), QUAD)],
                                    ALU.mult).then_inc(logit_done[n], QUAD)

            run_layers(dve, [(4, NORM_LAG[0], step0, 2), (2, NORM_LAG[1], step1, 1),
                             (0, NORM_LAG[2], lambda s: gate_steps(2, D, s), 1),
                             (0, NORM_LAG[3], lambda s: gate_steps(3, ATT, s), 1)])

        @block.tensor
        def _(pe):
            pe.wait_ge(ident_ready, 4)
            pe.wait_ge(w0_loaded, 32)

            for c in range(C):
                for half in range(2):
                    for o in range(2):
                        at = half * D + o * P
                        t = nc.tensor.transpose(bank[6 + c][:, at:at + P],
                                                w0_nat[:, o, half * D + c * P:half * D + (c + 1) * P], ident[:])
                t.then_inc(w0_turned, 1)
            nc.tensor.transpose(bank[5][:, 0:G], mask_nat[0:G, :], ident[0:G, 0:G]).then_inc(prep_pe, 1)

            def prepare(s):
                if s.at(3):
                    pe.wait_ge(w_loaded, 16 * N_LOADS)
                    pe.wait_ge(prep_dve, 3)
                    nc.tensor.matmul(bank[6][:], ones_row[:], rows[:, 0:2 * D], start=True, stop=True)\
                        .then_inc(prep_pe, 1)
                if s.at(4):
                    pe.wait_ge(prep_dve, BIAS_STEP)
                    nc.tensor.matmul(bank[7][:], ones_row[:], rows[:, 2 * D:4 * D], start=True, stop=True)\
                        .then_inc(prep_pe, 1)
                if s.at(5):
                    pe.wait_ge(prep_act, 5)
                    nc.tensor.matmul(bank[6][:, 0:2], ones_row[:], rows[:, 4 * D:4 * D + 2], start=True,
                                     stop=True).then_inc(prep_pe, 1)
                for half in range(2):
                    if s.at(6 + half):
                        pe.wait_ge(prep_act, 6 + half)
                        for a in range(2):
                            for c in range(C):
                                at = a * D + c * P
                                t = nc.tensor.transpose(bank[7 - half][:, at:at + P],
                                                        wqk2_nat[:, c, half * D + a * P:half * D + (a + 1) * P],
                                                        ident[:])
                        t.then_inc(prep_pe, 1)
                if s.at(8):
                    pe.wait_ge(prep_act, 8)
                    for c in range(C):
                        for o in range(2):
                            at = c * D + o * P
                            t = nc.tensor.transpose(bank[7][:, at:at + P], wv3_nat[:, o, c * P:(c + 1) * P],
                                                    ident[:])
                    t.then_inc(prep_pe, 1)
                if s.at(9):
                    pe.wait_ge(prep_act, 9)
                    for c in range(C):
                        t = nc.tensor.transpose(bank[6][:, c * P:(c + 1) * P], wqk3_nat[:, c * P:(c + 1) * P],
                                                ident[:])
                    t.then_inc(prep_pe, 1)
                if s.at(10):
                    pe.wait_ge(prep_act, 10)
                    for c in range(C):
                        for a in range(2):
                            t = nc.tensor.matmul(bank[7][:, c * D:(c + 1) * D],
                                                 wqk2_t[:, a, c * P:(c + 1) * P], wqk2_t[:, 2 + a, :],
                                                 start=(c == 0 and a == 0), stop=(a == 1),
                                                 skip_group_check=True)
                    t.then_inc(prep_pe, 1)

            def split_product(dst, left, right, first, last=True):
                for n, (a, b) in enumerate(((0, 0), (0, 1), (1, 0))):
                    m = nc.tensor.matmul(dst, left(a), right(b), start=first and n == 0, stop=last and n == 2,
                                         skip_group_check=True)
                return m

            def step0(s):
                if g := s.item(2):
                    wait(pe, x_fixed_done, g.count())
                    wait(pe, an_done, g.count())
                    wait(pe, xlo_done, g.count(2))
                    b = bank[g.ring(2)]
                    for c in range(C):
                        nc.tensor.transpose(b[:, c * P:(c + 1) * P], x_fixed[:, g.ring(4), c * P:(c + 1) * P],
                                            ident[:])
                    nc.tensor.transpose(b[:, D:D + P], an[:, g.ring(2), :], ident[:]).then_inc(tr0_done, 1)
                if s.at(-1):
                    pe.wait_ge(w0_ready, C)
                    pe.wait_ge(prep_act, 3)
                if g := s.item(1):
                    wait(pe, xlo_done, g.count())
                    wait(pe, relu0_done, g.count(4))
                    for c in range(C):
                        m = split_product(bank[2 + g.ring(4)][:],
                                          lambda h: xt0[:, g.ring(2), h, c * P:(c + 1) * P],
                                          lambda h: w0[h][:, c, :], c == 0, False)
                    m.then_inc(xw0_done, 1)
                if g := s.item(0):
                    wait(pe, y0_done, g.count())
                    nc.tensor.matmul(bank[2 + g.ring(4)][:, 0:D], at_f[:, g.ring(4), :], y0[:, g.ring(2), :],
                                     start=False, stop=True, skip_group_check=True).then_inc(ay_done, 1)
                prepare(s)


            def turn_x(n, g):
                wait(pe, lo_done[n], g.count())
                wait_back(pe, xt_done[n], g, 2, xlo_done if n == 1 else xt_done[n - 1])
                for h, part in enumerate((hi, lo)):
                    for c in range(C):
                        at = (2 * h + c) * P
                        t = nc.tensor.transpose(bank16[g.ring(2)][:, at:at + P],
                                                part[:, g.ring(4), c * P:(c + 1) * P], ident16[:])
                t.then_inc(trx_done[n], 1)

            def x_chunk(dst, g, w, a, b, c, first):
                return split_product(dst, lambda h: xt[:, g.ring(8), 2 * h + c, :],
                                     lambda h: w[h][:, c, a:b], first and c == 0, c == C - 1)

            def times_x(dst, g, w, a, b, first):
                for c in range(C):
                    m = x_chunk(dst, g, w, a, b, c, first)
                return m

            def step1(s):
                if g := s.item(0):
                    wait(pe, tlo_done, g.count())
                    wait(pe, tt_done, g.count(2))
                    for h in range(2):
                        t = nc.tensor.transpose(bank16[6 + g.ring(2)][:, h * P:(h + 1) * P],
                                                tr[:, g.ring(2), h, :], ident16[:])
                    t.then_inc(trt_done, 1)
                if s.at(-3):
                    pe.wait_ge(prep_act, PREP_ACT)
                    pe.wait_ge(prep_dve, PREP_DVE)
                if g := s.item(3):
                    turn_x(1, g)
                if g := s.item(2):
                    b = bank[2 + g.ring(2)]
                    wait(pe, xt_done[1], g.count())
                    if s.at(-2) or s.at(-1):
                        pe.wait_ge(relu0_done, G - 3 + g.index)
                    wait(pe, ylo_done, g.count(2))
                    times_x(b[:, 0:D + 2], g, w1, 2 * D, 3 * D + 2, True).then_inc(xwb_done, 1)
                if g := s.item(0):
                    wait(pe, tt_done, g.count())
                    wait(pe, ylo_done, g.count())
                    split_product(bank[4 + g.ring(2)][:, D:2 * D], lambda h: tr_t[:, g.ring(2), h, :],
                                  lambda h: yh[:, g.ring(2), h, :], False).then_inc(ty_done, 1)
                for c in range(C):
                    if g := s.item(1):
                        wait_back(pe, relu_done, g, 2, relu0_done)
                        x_chunk(bank[4 + g.ring(2)][:], g, w1, 0, 2 * D, c, True)
                    if c == 0 and (g := s.item(2)):
                        wait(pe, sjlo_done, g.count())
                        for h in range(2):
                            m = nc.tensor.matmul(bank[2 + g.ring(2)][:, D + 2:D + 2 + P],
                                                 sj[:, g.ring(2), h:h + 1].to_broadcast([P, P]), ident_s[:],
                                                 start=False, stop=(h == 1), skip_group_check=True)
                        m.then_inc(sj_spread, 1)
                if g := s.item(1):
                    nc.tensor.matmul(bank[4 + g.ring(2)][:, 0:D], ones1[:], bias1[:], start=False, stop=False,
                                     skip_group_check=True).then_inc(xwa_done, 1)
                if g := s.item(0):
                    wait(pe, zlo_done, g.count())
                    split_product(bank[4 + g.ring(2)][:, 0:D], lambda h: tr_t[:, g.ring(2), h, :],
                                  lambda h: zh[:, g.ring(2), h, :], False).then_inc(tz_done, 1)

            def gate_steps(n, s):
                if (g := s.item(-4)) and g.pos % QUAD == QUAD - 1:
                    wait(pe, prow_done[n], g.count())
                    nc.tensor.matmul(bank[7][:, P:P + QUAD], prow[:, g.ring(8) // QUAD, :],
                                     ident[0:QUAD, 0:QUAD], start=True, stop=True).then_inc(pback[n], QUAD)
                if g := s.item(1 - RES_LAG[n]):
                    wait_back(pe, res_done[n], g, 2, relu_done if n == 2 else res_done[n - 1])
                    a = D if n == 2 else P
                    times_x(bank[4 + g.ring(2)][:, 0:D], g, w2 if n == 2 else w3, a, a + D, True)\
                        .then_inc(v_done[n], 1)
                if g := s.item(0):
                    b = bank[2 + g.ring(2)]
                    if n == 2:
                        wait(pe, q_saved[n], g.count())
                        split_product(b[:, D:2 * D], lambda h: am_t[:, g.index, h, :],
                                      lambda h: (hi, lo)[h][:, g.ring(4), :], False).then_inc(ax_done[2], 1)
                    else:
                        wait(pe, klo_done, g.count())
                        split_product(b[:, D:D + ATT], lambda h: an_t[:, g.index, h, :],
                                      lambda h: kh[:, g.ring(2), h, :], False).then_inc(ax_done[3], 1)
                if g := s.item(1):
                    wait(pe, xt_done[n], g.count())
                    wait_back(pe, dot_done[n], g, 2, ylo_done if n == 2 else dot_done[n - 1])
                    width = D if n == 2 else 2 * ATT
                    times_x(bank[2 + g.ring(2)][:, 0:width], g, w2 if n == 2 else w3, 0, width, True)\
                        .then_inc(qx_done[n], 1)
                if g := s.item(2):
                    turn_x(n, g)
                if (g := s.item(-1)) and g.pos % QUAD == QUAD - 1:
                    wait(pe, logit_done[n], g.count())
                    wait_back(pe, pcol_done[n], g, 4, tt_done if n == 2 else pcol_done[n - 1])
                    nc.tensor.matmul(bank[7][0:QUAD, 0:P], logits[:, g.ring(8) // QUAD, :], ident[:],
                                     start=True, stop=True).then_inc(turned[n], QUAD)

            run_layers(pe, [(2, 0, step0, 2), (3, 0, step1, 1),
                            (2, RES_LAG[2] - 1, lambda s: gate_steps(2, s), 1),
                            (2, RES_LAG[3] - 1, lambda s: gate_steps(3, s), 1)])


_INPUTS = ["x", "adj", "nodemask", "L0_gnn_W", "L1_gnn_Wv", "L1_gnn_bv", "L1_gnn_aw", "L1_gnn_ab",
           "L1_gnn_Wk", "L1_gnn_bk", "L2_gnn_Wqk", "L2_gnn_Wv", "L3_gnn_W_qk", "L3_gnn_W_v"]


def kernel(**inputs):
    import numpy as np
    import concourse.bacc as bacc
    from concourse.bass_utils import run_bass_kernel_spmd

    nc = bacc.Bacc("TRN2", target_bir_lowering=False, num_devices=1)
    arrays, args = {}, []
    for name in _INPUTS:
        a = np.ascontiguousarray(inputs[name])
        if name == "L1_gnn_aw":
            a = a.reshape(-1)
        arrays[f"in_{name}"] = a
        args.append(nc.dram_tensor(f"in_{name}", a.shape, mybir.dt.from_np(a.dtype), kind="ExternalInput").ap())
    out = nc.dram_tensor("out_x", (G, P, D), F32, kind="ExternalOutput").ap()
    gnn_stack(nc, *args, out)
    result = run_bass_kernel_spmd(nc, [arrays], core_ids=[0])
    return result.results[0]["out_x"]
```
